# Optimizing a Trainium2 kernel written in Bass

```python
import numpy as np
import jax
import jax.numpy as jnp

def _softmax(x, axis=-1):
    return jax.nn.softmax(x, axis=axis)

def _gelu(x):
    return jax.nn.gelu(x, approximate=True)

def _silu(x):
    return jax.nn.silu(x)

def _sigmoid(x):
    return jax.nn.sigmoid(x)

def _layernorm(x, axis=-1, eps=1e-05):
    m = jnp.mean(x, axis=axis, keepdims=True)
    v = jnp.var(x, axis=axis, keepdims=True)
    return (x - m) / jnp.sqrt(v + eps)

def _scatter_add(tgt, idx, src, axis=0):
    return tgt.at[idx].add(src)

def _segment_sum(src, seg, n):
    return jax.ops.segment_sum(src, seg, n)
kernel_name = 'mk_xattn_ffn_d1_seqx_r4_6b9e56'

def setup_inputs(seed: int=0):
    np.random.seed(seed)
    _w = jnp.asarray

    def _rec_inputs():
        import jax
        import jax.numpy as jnp
        _rk = jax.random.key(seed)
        x = 7.22e-05 + 1 * jax.random.normal(jax.random.fold_in(_rk, 1), (4, 1024, 256), jnp.float32)
        _lenS = 1024 - jax.random.randint(jax.random.fold_in(_rk, 7), (4,), 0, max(1, 1024 // 4) + 1, jnp.int32)
        _lenS2 = 154 - jax.random.randint(jax.random.fold_in(_rk, 8), (4,), 0, max(1, 154 // 4) + 1, jnp.int32)
        _ctx_1024P = jax.random.normal(jax.random.fold_in(_rk, 11), (4, 16, 256), jnp.float32)
        _ctx_1024c = jax.random.dirichlet(jax.random.fold_in(_rk, 511), 0.3 * jnp.ones((16,), jnp.float32), (4, 154))
        _ctx_1024t = jnp.einsum('bsk,bkd->bsd', _ctx_1024c, _ctx_1024P)
        _ctx_1024t = _ctx_1024t * jax.lax.rsqrt(jnp.mean(jnp.square(_ctx_1024t)) + 1e-12) * 0.953939
        ctx_1024 = 4.13588e-05 + 0.999923 * (_ctx_1024t + 0.3 * jax.random.normal(jax.random.fold_in(_rk, 611), (4, 154, 256), jnp.float32))
        return (x, ctx_1024)
    x, ctx_1024 = _rec_inputs()

    def _L0_xattn_setup():
        import jax, jax.numpy as jnp
        import numpy as np
        B, L1, L2 = (4, 512, 512)
        INP1_DIM = INP2_DIM = 256
        QK_DIM = V_DIM = 256
        HEAD_N = 16
        QK_HEAD = QK_DIM // HEAD_N
        V_HEAD = V_DIM // HEAD_N
        SCALE = 1.0 / QK_HEAD ** 0.5

        def _linear_params(key, out_dim, in_dim):
            kw, kb = jax.random.split(key)
            bound = 1.0 / np.sqrt(in_dim)
            W = jax.random.uniform(kw, (out_dim, in_dim), jnp.float32, -bound, bound)
            b = jax.random.uniform(kb, (out_dim,), jnp.float32, -bound, bound)
            return (W, b)
        key = jax.random.key(seed)
        k1, k2, kq, kk, kv = jax.random.split(key, 5)
        inp1 = jax.random.normal(k1, (B, L1, INP1_DIM), jnp.float32)
        inp2 = jax.random.normal(k2, (B, L2, INP2_DIM), jnp.float32)
        Wq, bq = _linear_params(kq, QK_DIM, INP1_DIM)
        Wk, bk = _linear_params(kk, QK_DIM, INP2_DIM)
        Wv, bv = _linear_params(kv, V_DIM, INP2_DIM)
        return {'inp1': inp1, 'inp2': inp2, 'Wq': Wq, 'bq': bq, 'Wk': Wk, 'bk': bk, 'Wv': Wv, 'bv': bv, 'rescale_with_score': 1}
    _L0_xattn_all = _L0_xattn_setup()
    _L0_xattn_in = {k: v for k, v in _L0_xattn_all.items() if k in ('Wq', 'bq', 'Wk', 'bk', 'Wv', 'bv')}
    del _L0_xattn_all

    def _L0_ffn_setup():
        import jax, jax.numpy as jnp
        import numpy as np
        from math import ceil
        CAPACITY_FACTOR = 2.0
        MIN_CAPACITY = 4
        key = jax.random.key(seed)
        ks = jax.random.split(key, 4)
        B, S, D, Di, E = (4, 512, 256, 1024, 8)
        x = jax.random.normal(ks[0], (B, S, D), dtype=jnp.float32)
        Wr = jax.random.normal(ks[1], (D, E), dtype=jnp.float32) * D ** (-0.5)
        W1 = jax.random.normal(ks[2], (E, D, Di), dtype=jnp.float32) * D ** (-0.5)
        b1 = jnp.zeros((E, Di), dtype=jnp.float32)
        W2 = jax.random.normal(ks[3], (E, Di, D), dtype=jnp.float32) * Di ** (-0.5)
        b2 = jnp.zeros((E, D), dtype=jnp.float32)
        return {'x': x, 'Wr': Wr, 'W1': W1, 'b1': b1, 'W2': W2, 'b2': b2}
    _L0_ffn_all = _L0_ffn_setup()
    _L0_ffn_in = {k: v for k, v in _L0_ffn_all.items() if k in ('Wr', 'W1', 'b1', 'W2', 'b2')}
    del _L0_ffn_all
    return {'x': x, 'ctx_1024': ctx_1024, 'L0_xattn_Wq': _L0_xattn_in['Wq'], 'L0_xattn_bq': _L0_xattn_in['bq'], 'L0_xattn_Wk': _L0_xattn_in['Wk'], 'L0_xattn_bk': _L0_xattn_in['bk'], 'L0_xattn_Wv': _L0_xattn_in['Wv'], 'L0_xattn_bv': _L0_xattn_in['bv'], 'L0_ffn_Wr': _L0_ffn_in['Wr'], 'L0_ffn_W1': _L0_ffn_in['W1'], 'L0_ffn_b1': _L0_ffn_in['b1'], 'L0_ffn_W2': _L0_ffn_in['W2'], 'L0_ffn_b2': _L0_ffn_in['b2']}

def reference(x, ctx_1024, L0_xattn_Wq, L0_xattn_bq, L0_xattn_Wk, L0_xattn_bk, L0_xattn_Wv, L0_xattn_bv, L0_ffn_Wr, L0_ffn_W1, L0_ffn_b1, L0_ffn_W2, L0_ffn_b2):
    import jax
    import jax.numpy as jnp

    def _L0_xattn_ref(inp1, inp2, Wq, bq, Wk, bk, Wv, bv, rescale_with_score):
        import jax, jax.numpy as jnp
        import numpy as np
        B, L1, L2 = (4, 512, 512)
        INP1_DIM = INP2_DIM = 256
        QK_DIM = V_DIM = 256
        HEAD_N = 16
        QK_HEAD = QK_DIM // HEAD_N
        V_HEAD = V_DIM // HEAD_N
        SCALE = 1.0 / QK_HEAD ** 0.5

        def _linear_params(key, out_dim, in_dim):
            kw, kb = jax.random.split(key)
            bound = 1.0 / np.sqrt(in_dim)
            W = jax.random.uniform(kw, (out_dim, in_dim), jnp.float32, -bound, bound)
            b = jax.random.uniform(kb, (out_dim,), jnp.float32, -bound, bound)
            return (W, b)
        b, l1, _ = inp1.shape
        l2 = inp2.shape[1]
        q = (jnp.einsum('bld,ed->ble', inp1, Wq) + bq).reshape(b, l1, HEAD_N, QK_HEAD)
        k = (jnp.einsum('bmd,ed->bme', inp2, Wk) + bk).reshape(b, l2, HEAD_N, QK_HEAD)
        v = (jnp.einsum('bmd,ed->bme', inp2, Wv) + bv).reshape(b, l2, HEAD_N, V_HEAD)
        s = jax.nn.softmax(jnp.einsum('blhd,bmhd->blmh', q, k) * SCALE, axis=2)
        res = jnp.einsum('blmh,bmhd->blhd', s, v)
        if rescale_with_score:
            denom = jnp.sqrt(jnp.sum(s * s, axis=2))[..., None]
            res = res / denom
        return res.reshape(b, l1, -1)

    def _L0_ffn_ref(x, Wr, W1, b1, W2, b2):
        import jax, jax.numpy as jnp
        import numpy as np
        from math import ceil
        CAPACITY_FACTOR = 2.0
        MIN_CAPACITY = 4
        B, S, D = x.shape
        E = Wr.shape[1]
        N = B * S
        k = max(MIN_CAPACITY, ceil(N * CAPACITY_FACTOR / E))
        xt = x.reshape(N, D)
        scores = jax.nn.softmax(xt @ Wr, axis=-1)
        G, idx = jax.lax.top_k(scores.T, k)
        X_in = xt[idx]
        h = jax.nn.gelu(jnp.einsum('ekd,edh->ekh', X_in, W1) + b1[:, None, :], approximate=False)
        X_e = jnp.einsum('ekh,ehd->ekd', h, W2) + b2[:, None, :]
        contrib = (G[..., None] * X_e).reshape(E * k, D)
        out = jnp.zeros((N, D), dtype=x.dtype).at[idx.reshape(-1)].add(contrib)
        return out.reshape(B, S, D)
    x = x + _L0_xattn_ref(_layernorm(x, axis=-1), ctx_1024, L0_xattn_Wq, L0_xattn_bq, L0_xattn_Wk, L0_xattn_bk, L0_xattn_Wv, L0_xattn_bv, 1)
    x = x + _L0_ffn_ref(_layernorm(x, axis=-1), L0_ffn_Wr, L0_ffn_W1, L0_ffn_b1, L0_ffn_W2, L0_ffn_b2)
    return x

_drawn_inputs = setup_inputs


def setup_inputs(seed=0):
    import zlib

    import numpy as np

    out = dict(_drawn_inputs(seed))
    spreads = {'L0_ffn_b1': (0.0, 0.8), 'L0_ffn_b2': (0.0, 0.649)}
    factors = {'L0_xattn_bq': 6.439, 'L0_xattn_bk': 8.0}
    for name, (base, spread) in spreads.items():
        noise = np.random.default_rng([zlib.crc32(name.encode()), seed]).standard_normal(out[name].shape)
        drawn = base * np.exp(spread * noise) if base else spread * noise
        out[name] = jnp.asarray(drawn.astype(out[name].dtype))
    for name, factor in factors.items():
        out[name] = (out[name] * factor).astype(out[name].dtype)
    return out
```

```python
import numpy as np
import concourse.bass as bass
from concourse import mybir
from contextlib import ExitStack

B, L1, L2, D = 4, 1024, 154, 256
H, DH = 16, 16
NE, DI, CAP = 8, 1024, 1024
P = 128
N = B * L1
CT = 512
TPC = CT // P
NCH = N // CT
NT = N // P
KD = D // P
REM = L2 - P
HPT = P // DH
NPAIR = H // 2
NQUAD = H // 4
MT = DI // P
ST = CAP // P
EPS = 1e-5
SCALE = 1.0 / DH ** 0.5
RSQRT_SEED = 0x5F3759DF
FIRST_LOADS = 11
EXPERT_STEPS = 19
PIECES = 8
LISTS_AT = 6
HOTS = 4
PRIMED = {"logits_ready": 1, "x2T_ready": 1, "x2n_stored": 16}
DVE_STEPS = 38
ROUNDS = 8
SHIFTS = [26, 22, 18, 14, 10, 6, 2, 0]
MAX_GROUPS = [(0, 3), (3, 3), (6, 2)]

C_IDENT, C_ONES, C_BLOCK = 0, 128, 256
C_HALF = 384
C_HEAD = C_HALF + 2
C_ESC = C_HEAD + HPT
C_FIRST = C_ESC + 1
C_SUM = C_FIRST + NE
C_VR = C_SUM + 32
C_ALL = C_VR + H * 32
B_TRI, B_ONES, B_IOTA, B_TOK = 0, 128, 256, 384
B_IOTA8 = B_TOK + NT * 2
B_ALL = B_IOTA8 + ST


def constants():
    p = np.arange(P)
    c = np.zeros((P, C_ALL), np.float32)
    c[:, C_IDENT:C_IDENT + P] = np.eye(P)
    c[:, C_ONES:C_ONES + P] = 1
    c[:, C_BLOCK:C_BLOCK + P] = p[:, None] // 16 == p[None] // 16
    for s in range(2):
        c[:, C_HALF + s] = (p % 32) // 16 == s
    for j in range(HPT):
        c[:, C_HEAD + j] = p // DH == j
    c[:, C_ESC] = np.where((p // 32) % 2 == 0, SCALE, 2 * SCALE)
    for e in range(NE):
        c[16 * e, C_FIRST + e] = 1
    c[:, C_SUM + DH] = 1
    vr = np.zeros((P, H, 32), np.float32)
    vr[32:32 + REM, 0::2, DH] = 1
    vr[96:96 + REM, 1::2, DH] = 1
    c[:, C_VR:C_VR + H * 32] = vr.reshape(P, -1)
    ks = np.zeros((P, NPAIR, 3 * P), np.float32)
    for h in range(H):
        i, s = h // 2, h % 2
        for row in (96 + h, 112 + h):
            ks[row, i, s * P:(s + 1) * P] = 1
            for at in (0, 32):
                ks[row, i, 2 * P + 64 * s + at:2 * P + 64 * s + at + REM] = 1
    b = np.zeros((P, B_ALL), np.float32)
    b[:, B_TRI:B_TRI + P] = p[:, None] < p[None]
    b[:, B_ONES:B_ONES + P] = 1
    b[:, B_IOTA:B_IOTA + P] = p[None]
    b[:, B_TOK:B_TOK + 2 * NT:2] = p[:, None]
    b[:, B_TOK + 1:B_TOK + 2 * NT:2] = np.arange(NT)[None]
    b[:, B_IOTA8:] = np.arange(ST)[None]
    j = p % 16
    bits = np.stack([(j << s) if s else (j & 3) for s in SHIFTS], 1).astype(np.int32)
    return c, b, bits, ks[96:].reshape(32, -1)


class Tally:

    def __init__(self, engine, per_batch):
        self.engine, self.per_batch, self.trip = engine, per_batch, None
        self.n = dict(PRIMED)

    def add(self, sem, k=1):
        name = sem if isinstance(sem, str) else sem.name
        self.n[name] = self.n.get(name, 0) + k
        return self.n[name]

    def wait(self, sem, value):
        if self.trip is not None:
            assert value > 0, sem.name
            self.engine.wait_ge(sem, self.trip * self.per_batch[sem.name] + value)
        elif value > 0:
            self.engine.wait_ge(sem, value)

    def next(self, sem, k=1):
        self.wait(sem, self.add(sem, k))

    def loop(self, first, end, body):
        before = dict(self.n)
        with self.engine.Fori(0, end - first) as trip:
            self.trip = trip
            body(trip + first)
            self.trip = None
        for name, n in self.n.items():
            d = n - before.get(name, 0)
            assert d == 0 or d == self.per_batch[name], (name, d, self.per_batch[name])
            self.n[name] = n + d * (end - first - 1)


def build_kernel(nc, x_d, ctx_d, wq_d, wk_d, wv_d, bq_d, bk_d, bv_d, wr_d, w1_d, b1_d, w2_d, b2_d,
                 cf_d, cb_d, ci_d, ck_d, out_d):
    f32, f32r, bf16 = mybir.dt.float32, mybir.dt.float32r, mybir.dt.bfloat16
    i32, u32 = mybir.dt.int32, mybir.dt.uint32
    ALU, ACT, AX = mybir.AluOpType, mybir.ActivationFunctionType, mybir.AxisListType.X
    ctx = ExitStack()
    with ctx:
        def sb(name, shape, dt, stack=ctx):
            return stack.enter_context(nc.sbuf_tensor(name, shape, dt))

        sems = {}

        def sem(name):
            sems[name] = ctx.enter_context(nc.semaphore(name))
            return sems[name]

        x2n_rows = nc.dram_tensor("x2n_rows", [N, D], f32, kind="Internal").ap()
        x_c = x_d.rearrange("(g t p) d -> g p t d", t=TPC, p=P)
        out_c = out_d.rearrange("(g t p) d -> g p t d", t=TPC, p=P)
        x2n_c = x2n_rows.rearrange("(g t p) d -> g p t d", t=TPC, p=P)

        cf = sb("cf", [P, C_ALL], f32)
        cb = sb("cb", [P, B_ALL], bf16)
        ci = sb("ci", [P, ROUNDS], i32)
        ident = cf[:, C_IDENT:C_IDENT + P]
        wr = sb("wr", [P, KD, NE], f32)
        b1 = sb("b1", [P, NE, MT], f32)
        logits = sb("logits", [P, NT, NE], f32)

        att = ExitStack()
        wq = sb("wq", [P, KD, D], f32, att)
        wk = sb("wk", [P, KD, D], f32, att)
        wv = sb("wv", [P, KD, D], f32, att)
        bq = sb("bq", [P, KD], f32, att)
        bk = sb("bk", [P, KD], f32, att)
        bv = sb("bv", [P, D], f32, att)
        idle = sb("idle", [P, 1], f32, att)
        eps = sb("eps", [P, TPC], f32, att)
        minus_half = sb("minus_half", [P, TPC], f32, att)
        ctxT = sb("ctxT", [P, KD, L2 + P], f32, att)
        xc = sb("xc", [P, 2, TPC, D], f32, att)
        xr = sb("xr", [P, TPC, D], f32, att)
        xn = sb("xn", [P, TPC, D], f32, att)
        xnT = sb("xnT", [P, KD, CT], f32, att)
        qhi = sb("qhi", [P, KD, CT], f32r, att)
        qlo = sb("qlo", [P, KD, CT], f32r, att)
        khi = sb("khi", [P, KD, L2], f32r, att)
        klo = sb("klo", [P, KD, L2], f32r, att)
        kst = [sb(f"kst{i}", [P, KD, 3 * P], f32r, att) for i in range(2)]
        kbd = sb("kbd", [P, KD, HPT, L2], f32r, att)
        qs = [sb(f"qs{i}", [P, NPAIR, CT], f32r, att) for i in range(2)]
        ks = sb("ks", [P, NPAIR, 3 * P], f32r, att)
        vst = sb("vst", [P, 2, D], f32, att)
        vmain = sb("vmain", [P, H, 32], f32, att)
        vrem = sb("vrem", [P, H, 32], f32, att)
        ex = sb("ex", [P, 12, CT], f32, att)
        sq = sb("sq", [P, 8, CT], f32, att)
        osb = sb("osb", [P, 2, NQUAD, CT], f32, att)
        maxes = sb("maxes", [P, TPC, H], f32, att)
        negmax = sb("negmax", [P, TPC, 2, H], f32r, att)
        negmaxT = sb("negmaxT", [32, CT], f32r, att)
        ot = sb("ot", [P, TPC * H, DH + 1], f32, att)
        res = sb("res", [P, TPC * H, DH], f32, att)
        x1 = sb("x1", [P, TPC, D], f32, att)
        x2n = sb("x2n", [P, TPC, D], f32, att)
        x2T = sb("x2T", [P, KD, CT], f32, att)
        bn = sb("bn", [P, 2, TPC, 6], f32, att)
        mv = sb("mv", [P, 2, TPC, 2], f32, att)
        veps = sb("veps", [P, 2, TPC], f32, att)
        rstd = sb("rstd", [P, 2, TPC], f32, att)
        rs = sb("rs", [P, TPC * H], f32, att)
        rt = sb("rt", [P, TPC * H], f32, att)
        ri = sb("ri", [P, TPC * H], i32, att)
        att.close()

        slot_lo = sb("slot_lo", [P, NE, NT], f32)
        slot_hi = sb("slot_hi", [P, NE, NT], bf16)
        gate3 = sb("gate3", [P, NE, NT, 3], bf16)
        w1raw = sb("w1raw", [P, KD * DI], f32)
        w2raw = sb("w2raw", [P, MT * D], f32)
        w1s = [sb(f"w1s{i}", [P, KD * DI], f32r) for i in range(2)]
        b1c = sb("b1c", [P, MT], f32)
        b2c = sb("b2c", [P, D], f32)
        hot_hi = sb("hot_hi", [P, NT, ST], bf16)
        values = sb("values", [P, NT, ST, 5], bf16)
        packed = sb("packed", [P, ST, 5], f32)
        tok_next = sb("tok_next", [P, ST], u32)
        tok_now = sb("tok_now", [P, ST], u32)
        gate_next = sb("gate_next", [P, ST], f32)
        gate_now = sb("gate_now", [P, ST], f32)
        carrier = sb("carrier", [P, 2], f32)

        routing = ExitStack()
        scores = sb("scores", [P, NE, NT], f32, routing)
        scoresT = sb("scoresT", [P, N], f32, routing)
        copies = sb("copies", [P, NT, P], f32, routing)
        above = sb("above", [P, N], bf16, routing)
        gate_rest = sb("gate_rest", [P, NE, NT], f32, routing)
        fresh = sb("fresh", [P, NE * NT], f32, routing)
        cum = sb("cum", [P, NE, NT], bf16, routing)
        cum_over = sb("cum_over", [P, NE, NT], bf16, routing)
        over = sb("over", [P, NE, NT], bf16, routing)
        same = sb("same", [P, NE, NT], bf16, routing)
        taken = sb("taken", [P, NE, NT], bf16, routing)
        before = sb("before", [P, NE, NT], bf16, routing)
        slot = sb("slot", [P, 3, NE, NT], i32, routing)
        exps = sb("exps", [P, NE, NT], f32, routing)
        best = sb("best", [P, 3, NT], f32, routing)
        found = sb("found", [P, 3], i32, routing)
        count = sb("count", [P, 2], f32, routing)
        wide = sb("wide", [P, P], f32, routing)
        thr = sb("thr", [P, NE], f32, routing)
        need = sb("need", [P, NE], f32, routing)
        routing.close()

        w2s = [sb(f"w2s{i}", [P, MT * D], f32r) for i in range(2)]
        xt = [sb(f"xt{i}", [P, KD, CAP], f32r) for i in range(2)]
        hid = [sb(f"hid{i}", [P, MT, CAP], f32r) for i in range(2)]
        hact = sb("hact", [P, 4, CT], f32)
        xg = sb("xg", [P, ST, D], f32)
        y = sb("y", [P, ST, D], f32)
        hot_lo = sb("hot_lo", [P, NT, P], bf16)

        bank = [ctx.enter_context(nc.psum_tensor(f"bank{i}", [P, 512], f32)) for i in range(8)]
        MAXB, SCB, OB, MISC = bank[0:2], bank[2:5], bank[5], bank[6:8]
        HIDB = [bank[i] for i in (0, 1, 2, 5)]
        YB, TURNB, LISTB = bank[3:5], bank[5:7], bank[7]

        first_in = sem("first_in")
        ks_const_in = sem("ks_const_in")
        ks_const = sem("ks_const")
        vrem_const = sem("vrem_const")
        kst_clear = sem("kst_clear")
        xc_in = [sem("xc_in0"), sem("xc_in1")]
        xr_in = sem("xr_in")
        ctx_in = sem("ctx_in")
        ln1_stats = sem("ln1_stats")
        ln1_rstd = sem("ln1_rstd")
        xn_ready = sem("xn_ready")
        xnT_ready = sem("xnT_ready")
        misc_full = [sem("misc_full0"), sem("misc_full1")]
        khi_ready = sem("khi_ready")
        klo_ready = sem("klo_ready")
        logits_ready = sem("logits_ready")
        kbd_ready = sem("kbd_ready")
        kst_ready = sem("kst_ready")
        ks_in = [sem(f"ks_in{i}") for i in range(NQUAD)]
        v_staged = sem("v_staged")
        v_ready = sem("v_ready")
        qhi_ready = sem("qhi_ready")
        qlo_ready = sem("qlo_ready")
        q_stacked = sem("q_stacked")
        max_full = sem("max_full")
        max_free = sem("max_free")
        negmax_ready = sem("negmax_ready")
        negmaxT_ready = sem("negmaxT_ready")
        m_stacked = sem("m_stacked")
        score_full = sem("score_full")
        exp_done = sem("exp_done")
        sq_done = sem("sq_done")
        av_done = sem("av_done")
        o_copied = sem("o_copied")
        ot_ready = sem("ot_ready")
        rs_ready = sem("rs_ready")
        res_ready = sem("res_ready")
        x1_ready = sem("x1_ready")
        ln2_stats = sem("ln2_stats")
        ln2_rstd = sem("ln2_rstd")
        x2n_ready = sem("x2n_ready")
        x2T_ready = sem("x2T_ready")
        x1_stored = sem("x1_stored")
        x2n_stored = sem("x2n_stored")
        dve_step = sem("dve_step")
        pool_step = sem("pool_step")
        maxima_taken = sem("maxima_taken")
        exps_ready = sem("exps_ready")
        scores_ready = sem("scores_ready")
        copies_ready = sem("copies_ready")
        copies_turned = sem("copies_turned")
        scoresT_ready = sem("scoresT_ready")
        feasible = sem("feasible")
        counted = sem("counted")
        wide_ready = sem("wide_ready")
        thr_turned = sem("thr_turned")
        fresh_ready = sem("fresh_ready")
        same_ready = sem("same_ready")
        same_ranked = sem("same_ranked")
        taken_ready = sem("taken_ready")
        taken_ranked = sem("taken_ranked")
        slots_ready = sem("slots_ready")
        gates_split = sem("gates_split")
        w1_in = sem("w1_in")
        w2_in = sem("w2_in")
        b2_in = sem("b2_in")
        w1hi_ready = sem("w1hi_ready")
        w1lo_ready = sem("w1lo_ready")
        w2hi_ready = sem("w2hi_ready")
        w2lo_ready = sem("w2lo_ready")
        b1c_ready = sem("b1c_ready")
        hot_ready = sem("hot_ready")
        hot_hi_ready = sem("hot_hi_ready")
        values_ready = sem("values_ready")
        list_full = sem("list_full")
        list_ready = sem("list_ready")
        gathered = [sem("gathered0"), sem("gathered1")]
        x_turned = sem("x_turned")
        xhi_ready = sem("xhi_ready")
        xlo_ready = sem("xlo_ready")
        hidden_full = sem("hidden_full")
        gelu_done = sem("gelu_done")
        hid_ready = sem("hid_ready")
        y_full = sem("y_full")
        y_taken = sem("y_taken")
        y_ready = sem("y_ready")
        scattered = sem("scattered")
        carried = sem("carried")

        per_batch = {s.name: k for s, k in {
            xc_in[0]: 16, xc_in[1]: 16, xr_in: 32, ctx_in: 16, ln1_stats: 2, ln1_rstd: 2,
            xn_ready: 2, xnT_ready: 4, misc_full[0]: 13, misc_full[1]: 13,
            khi_ready: 2, klo_ready: 2, kbd_ready: 1, kst_ready: 1, logits_ready: 2,
            **{s: 16 * 6 for s in ks_in}, v_staged: 1, v_ready: 1, qhi_ready: 4, qlo_ready: 4,
            q_stacked: 2 * 16 * 12, max_full: 48, max_free: 48, negmax_ready: 2,
            negmaxT_ready: 2, m_stacked: 32, score_full: 48, exp_done: 48, sq_done: 32,
            av_done: 8, o_copied: 8, ot_ready: 8, rs_ready: 2, res_ready: 2, x1_ready: 2,
            ln2_stats: 2, ln2_rstd: 2, x2n_ready: 2, x2T_ready: 4, x1_stored: 32,
            x2n_stored: 32, dve_step: DVE_STEPS, pool_step: 4,
        }.items()} | {"quads": 2 * NQUAD}

        per_expert = {s.name: k for s, k in {
            w1_in: 16, w2_in: 16, b2_in: 16, w1hi_ready: PIECES, w1lo_ready: PIECES,
            w2hi_ready: PIECES, w2lo_ready: PIECES, b1c_ready: 1, hot_ready: HOTS,
            hot_hi_ready: 1, values_ready: 1, list_full: 1, list_ready: 1, gathered[0]: 8 * ST, gathered[1]: 8 * ST, x_turned: 4,
            xhi_ready: 4, xlo_ready: 4, hidden_full: 2 * MT, gelu_done: 2 * MT,
            hid_ready: 2 * MT, y_full: ST, y_taken: ST, y_ready: ST, scattered: 16 * ST,
            carried: 1 + ST, dve_step: EXPERT_STEPS,
        }.items()}

        def every_expert(tally, expert):
            tally.per_batch = per_expert
            expert(0, True)
            tally.loop(1, NE - 1, lambda e: expert(e, True))
            expert(NE - 1, False)

        def attention_over(engine):
            engine.wait_ge(logits_ready, NCH + PRIMED["logits_ready"])
            engine.wait_ge(x1_stored, 16 * NCH)
            engine.wait_ge(x2n_stored, 16 * NCH + PRIMED["x2n_stored"])

        def every_chunk(tally, chunk, straight=False):
            chunk(0, 0, 0, dict(prepare=True, finish=False, route=False, load=True))
            chunk(0, 1, 1, dict(prepare=True, finish=True, route=False, load=True))

            def batch(b):
                for c in range(2):
                    chunk(b, 2 * b + c, c, dict(prepare=True, finish=True, route=True, load=True))
            if straight:
                for b in range(1, B - 1):
                    batch(b)
            else:
                tally.loop(1, B - 1, batch)
            chunk(B - 1, NCH - 2, 0, dict(prepare=True, finish=True, route=True, load=False))
            chunk(B - 1, NCH - 1, 1, dict(prepare=False, finish=True, route=True, load=False))

        TILES = [(i, part) for i in range(2) for part in range(3)]

        block = ctx.enter_context(nc.Block())

        @block.sync
        def _(sp):
            tally = Tally(sp, per_batch)

            def load_x(g, parity):
                sp.dma_start(xc[:, parity], x_c[g]).then_inc(xc_in[parity], 16)

            def stack_queries(parity):
                tally.next(qhi_ready, KD)
                tally.next(qlo_ready, KD)
                for r in range(4):
                    for at, src in ((0, qhi), (32, qlo), (64, qhi)):
                        sp.dma_start(qs[parity][at:at + 32, r::4, :].bitcast(f32),
                                     src[32 * r:32 * r + 32, :, :].bitcast(f32)).then_inc(q_stacked, 16)

            def stack_maxima(parity):
                tally.next(negmaxT_ready)
                sp.dma_start(qs[parity][96:128, :, :].bitcast(f32),
                             negmaxT[:, :].bitcast(f32).rearrange("p (a c) -> p a c", a=1)
                             .broadcast_to([32, NPAIR, CT])).then_inc(m_stacked, 16)

            def stack_keys(quad):
                for i in (2 * quad, 2 * quad + 1):
                    et, r = i // 4, i % 4
                    for at, src in ((0, kst[0]), (32, kst[0]), (64, kst[1])):
                        sp.dma_start(ks[at:at + 32, i, :].bitcast(f32),
                                     src[32 * r:32 * r + 32, et, :].bitcast(f32))\
                          .then_inc(ks_in[quad], 16)

            def load_context(b):
                sp.dma_start(ctxT[:, :, :], ctx_d[b].rearrange("(k p) n -> p k n", p=P))\
                  .then_inc(ctx_in, 16)

            load_x(0, 0)
            sp.dma_start(cf[:, :], cf_d).then_inc(first_in, 16)
            for w, src in ((wk, wk_d), (wv, wv_d), (wq, wq_d)):
                sp.dma_start(w[:, :, :], src.rearrange("(k p) e -> p k e", p=P))\
                  .then_inc(first_in, 16)
            load_context(0)
            for w, src in ((bq, bq_d), (bk, bk_d)):
                sp.dma_start(w[:, :], src).then_inc(first_in, 16)
            sp.dma_start(bv[:, :], bv_d.rearrange("(a n) -> a n", a=1).broadcast_to([P, D]))\
              .then_inc(first_in, 16)
            sp.dma_start(osb[:, 0, 0, 0:B_ALL], cb_d).then_inc(first_in, 16)
            sp.dma_start(ci[:, :], ci_d).then_inc(first_in, 16)
            sp.dma_start(wr[:, :, :], wr_d.rearrange("(k p) e -> p k e", p=P)).then_inc(first_in, 16)
            sp.dma_start(b1[:, :, :], b1_d).then_inc(first_in, 16)
            sp.dma_start(sq[96:128, 0:6, :].rearrange("p a c -> p (a c)"), ck_d)\
              .then_inc(ks_const_in, 16)
            load_x(1, 1)
            stack_queries(0)
            tally.next(kst_ready)
            for quad in range(NQUAD):
                stack_keys(quad)
            stack_maxima(0)

            def chunk(b, g, parity, has):
                before = tally.n.get("score_full", 0)
                tally.add(xn_ready)
                if has["load"]:
                    tally.wait(xn_ready, tally.n["xn_ready"])
                    load_x(g + 2, parity)
                if has["finish"]:
                    if has["route"]:
                        tally.next(x1_ready)
                    sp.dma_start(xr[:, :, :], x_c[g - 1]).then_inc(xr_in, 16)
                if has["route"]:
                    sp.dma_start(out_c[g - 2], x1[:, :, :]).then_inc(x1_stored, 16)
                if parity == 0:
                    tally.next(v_staged)
                    if has["load"]:
                        load_context(b + 1)
                if has["prepare"]:
                    tally.wait(score_full, before)
                    stack_queries(1 - parity)
                tally.add(score_full, 24)
                if has["route"]:
                    tally.next(x2n_ready)
                    sp.dma_start(x2n_c[g - 2], x2n[:, :, :]).then_inc(x2n_stored, 16)
                if has["prepare"]:
                    if parity == 1:
                        tally.next(kst_ready)
                        for quad in range(NQUAD - 1):
                            tally.wait(score_full, before + 6 * (quad + 1))
                            stack_keys(quad)
                    stack_maxima(1 - parity)
                    if parity == 1:
                        tally.wait(score_full, before + 24)
                        stack_keys(NQUAD - 1)

            every_chunk(tally, chunk, straight=True)
            for g in (NCH - 2, NCH - 1):
                tally.next(x1_ready)
                if g == NCH - 2:
                    sp.dma_start(xr[:, :, :], x_c[NCH - 1]).then_inc(xr_in, 16)
                sp.dma_start(out_c[g], x1[:, :, :]).then_inc(x1_stored, 16)
                tally.next(x2n_ready)
                sp.dma_start(x2n_c[g], x2n[:, :, :]).then_inc(x2n_stored, 16)

            def load_w1(e):
                sp.dma_start(w1raw[:, :].rearrange("p (k n) -> p k n", k=KD),
                             w1_d[e].rearrange("(k p) n -> p k n", p=P)).then_inc(w1_in, 16)

            def load_w2(e):
                sp.dma_start(w2raw[:, :].rearrange("p (m n) -> p m n", m=MT),
                             w2_d[e].rearrange("(m p) n -> p m n", p=P)).then_inc(w2_in, 16)

            def load_b2(e):
                sp.dma_start(b2c[:, :], b2_d[e:e + 1, :].broadcast_to([P, D])).then_inc(b2_in, 16)

            attention_over(sp)
            load_w1(0)
            load_w2(0)
            load_b2(0)
            for e in range(1, NE):
                tally.next(w1hi_ready, PIECES)
                tally.next(w1lo_ready, PIECES)
                load_w1(e)
                tally.next(w2hi_ready, PIECES)
                tally.next(w2lo_ready, PIECES)
                load_w2(e)
                tally.next(y_taken, ST)
                load_b2(e)
            sp.wait_ge(scattered, NE * ST * 16)

        @block.scalar
        def _(act):
            tally = Tally(act, per_batch)

            def take(k):
                tally.next(misc_full[k])
                return MISC[k]

            def project_keys():
                filled = take(0)
                tally.wait(kst_ready, tally.add(kst_ready) - 1)
                for et in range(KD):
                    act.activation(khi[:, et, :], filled[:, et * 256:et * 256 + L2], ACT.Identity,
                                   bias=bk[:, et:et + 1]).then_inc(khi_ready, 1)
                    tally.add(khi_ready)

            def project_values():
                filled = take(1)
                tally.wait(v_ready, tally.add(v_staged) - 1)
                act.activation(vst[:, :, :], filled[:, :].rearrange("p (a e) -> p a e", a=2),
                               ACT.Copy).then_inc(v_staged, 1)

            def norm_turned():
                for d in range(KD):
                    act.activation(xnT[:, d, :], take(d)[:, :], ACT.Copy).then_inc(xnT_ready, 1)

            def queries():
                tally.wait(q_stacked, tally.n.get("q_stacked", 0))
                for et in range(KD):
                    act.activation(qhi[:, et, :], take(et)[:, :], ACT.Identity,
                                   bias=bq[:, et:et + 1]).then_inc(qhi_ready, 1)
                tally.add(q_stacked, 16 * 12)

            def maxima():
                filled = take(1)
                tally.wait(m_stacked, tally.n.get("m_stacked", 0))
                act.activation(negmaxT[:, :], filled[0:32, :], ACT.Copy).then_inc(negmaxT_ready, 1)
                tally.add(m_stacked, 16)

            def exponential(quad, n):
                i, part = TILES[n]
                if n == 0:
                    tally.wait(av_done, tally.add("quads") - 2)
                tally.next(score_full)
                scale = cf[:, C_ESC:C_ESC + 1] if part == 2 else SCALE
                act.activation(ex[:, (quad % 2) * 6 + n, :], SCB[n % 3][:, :], ACT.Exp, scale=scale)\
                   .then_inc(exp_done, 1)

            def outputs(quad, parity):
                tally.next(av_done)
                act.activation(osb[:, parity, quad, :], OB[:, :], ACT.Copy).then_inc(o_copied, 1)

            def outputs_turned(t):
                filled = take(t % 2)
                if t == 0:
                    tally.wait(res_ready, tally.add(res_ready) - 1)
                act.activation(ot[:, t * H:(t + 1) * H, :],
                               filled[:, :].rearrange("p (h r) -> p h r", r=32)[:, :, 0:DH + 1],
                               ACT.Copy).then_inc(ot_ready, 1)

            def route_turned():
                for d in range(KD):
                    act.activation(x2T[:, d, :], take(d)[:, :], ACT.Copy).then_inc(x2T_ready, 1)

            def router_logits(g):
                act.activation(logits[:, bass.ds(g * TPC, TPC), :],
                               take(0)[:, 0:TPC * NE].rearrange("p (t e) -> p t e", e=NE),
                               ACT.Copy).then_inc(logits_ready, 1)

            act.wait_ge(ks_const_in, 16)
            act.activation(ks[96:128, :, :].rearrange("p a c -> p (a c)"),
                           sq[96:128, 0:6, :].rearrange("p a c -> p (a c)"), ACT.Copy)\
               .then_inc(ks_const, 1)
            act.wait_ge(first_in, 16 * FIRST_LOADS)
            third = B_ALL // 3
            for i, s in enumerate((logits_ready, x2T_ready, x2n_stored)):
                act.activation(cb[:, i * third:(i + 1) * third], osb[:, 0, 0, i * third:(i + 1) * third],
                               ACT.Copy).then_inc(s, PRIMED[s.name])
            project_keys()
            project_values()
            norm_turned()
            queries()
            maxima()

            def chunk(b, g, parity, has):
                for slot in range(3 * NQUAD):
                    quad, r = slot // 3, slot % 3
                    if r == 0 and (quad >= 2 or has["finish"]):
                        outputs((quad + 2) % NQUAD, parity if quad >= 2 else 1 - parity)
                    for n in (2 * r, 2 * r + 1):
                        exponential(quad, n)
                    if has["prepare"]:
                        if slot == 0:
                            norm_turned()
                        if slot == 1:
                            queries()
                        if slot == 9:
                            maxima()
                    if has["route"] and slot == 3:
                        route_turned()
                    if has["finish"] and 4 <= slot < 4 + TPC:
                        outputs_turned(slot - 4)
                    if has["route"] and slot == 8:
                        router_logits(g - 2)
                    if parity == 0 and has["load"]:
                        if slot == 10:
                            project_keys()
                        if slot == 11:
                            project_values()

            every_chunk(tally, chunk)
            outputs(NQUAD - 2, 1)
            outputs(NQUAD - 1, 1)
            for t in range(TPC):
                outputs_turned(t)
            for g in (NCH - 2, NCH - 1):
                route_turned()
                router_logits(g)

            def split_w1():
                tally.next(w1_in, 16)
                n = KD * DI // PIECES
                for i in range(PIECES):
                    act.activation(w1s[0][:, i * n:(i + 1) * n], w1raw[:, i * n:(i + 1) * n],
                                   ACT.Copy).then_inc(w1hi_ready, 1)

            attention_over(act)
            act.wait_ge(maxima_taken, 1)
            act.activation(exps[:, :, :], scores[:, :, :], ACT.Exp).then_inc(exps_ready, 1)
            act.wait_ge(scores_ready, 1)
            for k in range(1, NCH, 2):
                act.activation(copies[:, k * TPC:(k + 1) * TPC, :]
                               .rearrange("p t (e j) -> p t e j", e=NE),
                               scores[:, :, k * TPC:(k + 1) * TPC].rearrange("p e (t a) -> p t e a", a=1)
                               .broadcast_to([P, TPC, NE, P // NE]), ACT.Copy).then_inc(copies_ready, 1)
            for k in range(1, NCH, 2):
                act.wait_ge(copies_turned, k + 1)
                act.activation(scoresT[:, k * CT:(k + 1) * CT], bank[k][:, :], ACT.Copy)\
                   .then_inc(scoresT_ready, 1)
            split_w1()

            def split_w2(i):
                if i == 0:
                    tally.next(w2_in, 16)
                n = MT * D // PIECES
                act.activation(w2s[0][:, i * n:(i + 1) * n], w2raw[:, i * n:(i + 1) * n],
                               ACT.Copy).then_inc(w2hi_ready, 1)

            def split_x(g):
                h, d = g // KD, g % KD
                tally.next(x_turned)
                act.activation(xt[0][:, d, h * CT:(h + 1) * CT], TURNB[g % 2][:, :], ACT.Copy)\
                   .then_inc(xhi_ready, 1)

            def expert(e, has_next):
                for k in range(2 * MT):
                    tally.next(hidden_full)
                    if k == 0:
                        tally.next(b1c_ready)
                    tally.wait(hid_ready, tally.add(hid_ready) - 4)
                    act.activation(hact[:, k % 4, :], HIDB[k % 4][:, :], ACT.Gelu,
                                   bias=b1c[:, k % MT:k % MT + 1]).then_inc(gelu_done, 1)
                    if 3 <= k < 3 + PIECES:
                        split_w2(k - 3)
                if has_next:
                    split_w1()
                    for g in range(4):
                        split_x(g)

            for g in range(4):
                split_x(g)
            every_expert(tally, expert)

        @block.tensor
        def _(pe):
            tally = Tally(pe, per_batch)

            def so_far(*events):
                for s in events:
                    tally.wait(s, tally.n.get(s.name, 0))

            def project_keys():
                tally.next(ctx_in, 16)
                so_far(ot_ready, klo_ready, logits_ready)
                for et in range(KD):
                    for d in range(KD):
                        last = pe.matmul(MISC[0][:, et * 256:et * 256 + L2],
                                         wk[:, d, et * P:(et + 1) * P], ctxT[:, d, 0:L2],
                                         start=(d == 0), stop=(d == KD - 1))
                last.then_inc(misc_full[0], 1)
                tally.add(klo_ready, KD)
                tally.add(kbd_ready)

            def project_values():
                so_far(v_staged, negmaxT_ready)
                for part, (a, b) in enumerate(((0, P), (L2, L2 + P))):
                    for d in range(KD):
                        last = pe.matmul(MISC[1][:, part * D:(part + 1) * D], ctxT[:, d, a:b],
                                         wv[:, d, :], start=(d == 0), stop=(d == KD - 1))
                last.then_inc(misc_full[1], 1)
                tally.add(v_staged)

            def turn(src, ready, k_ready, free):
                tally.next(ready)
                so_far(*free)
                for d in range(KD):
                    for t in range(TPC):
                        last = pe.transpose(MISC[d][:, t * P:(t + 1) * P],
                                            src[:, t, d * P:(d + 1) * P], ident)
                    last.then_inc(misc_full[d], 1)
                tally.add(k_ready, KD)

            def norm_turned():
                turn(xn, xn_ready, xnT_ready, (klo_ready, v_staged, ot_ready, logits_ready,
                                             negmaxT_ready))

            def queries():
                so_far(xnT_ready)
                for et in range(KD):
                    for d in range(KD):
                        last = pe.matmul(MISC[et][:, :], wq[:, d, et * P:(et + 1) * P],
                                         xnT[:, d, :], start=(d == 0), stop=(d == KD - 1))
                    last.then_inc(misc_full[et], 1)
                tally.add(qlo_ready, KD)

            GROUPS = [(t, et, j, n) for t in range(TPC) for et in range(KD) for j, n in MAX_GROUPS]

            def scores_for_maxima(first, end):
                for k in range(first, end):
                    t, et, j, n = GROUPS[k]
                    if k == 0:
                        tally.next(qhi_ready, KD)
                        tally.wait(kbd_ready, tally.n["kbd_ready"])
                    filled = tally.add(max_full)
                    tally.wait(max_free, filled - 2)
                    pe.matmul(MAXB[k % 2][:, 0:n * L2], qhi[:, et, t * P:(t + 1) * P],
                              kbd[:, et, j:j + n, :].rearrange("p j n -> p (j n)"),
                              start=True, stop=True).then_inc(max_full, 1)

            def maxima():
                tally.next(negmax_ready)
                so_far(x2T_ready, qlo_ready, ot_ready)
                for t in range(TPC):
                    last = pe.transpose(MISC[1][0:32, t * P:(t + 1) * P],
                                        negmax[:, t, :, :].rearrange("p a h -> p (a h)").bitcast(f32),
                                        ident)
                last.then_inc(misc_full[1], 1)
                tally.add(negmaxT_ready)

            def scores(quad, n, parity):
                i, part = TILES[n]
                pair = 2 * quad + i
                filled = tally.add(score_full)
                tally.wait(exp_done, filled - 3)
                pe.matmul(SCB[n % 3][:, :], ks[:, pair, part * P:(part + 1) * P],
                          qs[parity][:, pair, :], start=True, stop=True).then_inc(score_full, 1)

            def weighted(quad, r):
                base = tally.n.get("exp_done", 0)
                if r == 0:
                    tally.wait(o_copied, tally.n.get("o_copied", 0))
                for j in range(4):
                    h = 4 * quad + j
                    to = OB[32 * j:32 * j + 32, :]
                    if r == 0:
                        n = TILES.index((j // 2, j % 2))
                        tally.wait(exp_done, base + n + 1)
                        pe.matmul(to, vmain[:, h, :], ex[:, (quad % 2) * 6 + n, :], start=True,
                                  stop=False)
                    elif r == 1:
                        tally.next(sq_done)
                        pe.matmul(to, cf[:, C_SUM:C_SUM + 32], sq[:, (quad % 2) * 4 + j, :],
                                  start=False, stop=False)
                    else:
                        n = TILES.index((j // 2, 2))
                        tally.wait(exp_done, base + n + 1)
                        last = pe.matmul(to, vrem[:, h, :], ex[:, (quad % 2) * 6 + n, :],
                                         start=False, stop=True)
                if r == 2:
                    last.then_inc(av_done, 1)
                    tally.add(exp_done, 6)
                    tally.add(o_copied)

            def outputs_turned(t, parity):
                if t == 0:
                    so_far(o_copied, x2T_ready, qlo_ready)
                elif t == 1:
                    so_far(negmaxT_ready, x2T_ready)
                else:
                    tally.wait(ot_ready, tally.n["ot_ready"] - 1)
                for quad in range(NQUAD):
                    last = pe.transpose(MISC[t % 2][:, quad * P:(quad + 1) * P],
                                        osb[:, parity, quad, t * P:(t + 1) * P], ident)
                last.then_inc(misc_full[t % 2], 1)
                tally.add(ot_ready)

            def route_turned():
                turn(x2n, x2n_ready, x2T_ready, (qlo_ready, negmaxT_ready, logits_ready, ot_ready))

            def router_logits():
                so_far(x2T_ready, ot_ready)
                for t in range(TPC):
                    for d in range(KD):
                        last = pe.matmul(MISC[0][:, t * NE:(t + 1) * NE], x2T[:, d, t * P:(t + 1) * P],
                                         wr[:, d, :], start=(d == 0), stop=(d == KD - 1))
                last.then_inc(misc_full[0], 1)
                tally.add(logits_ready)

            pe.wait_ge(first_in, 16 * FIRST_LOADS)
            pe.wait_ge(ks_const, 1)
            project_keys()
            project_values()
            norm_turned()
            queries()
            scores_for_maxima(0, len(GROUPS))
            maxima()

            def chunk(b, g, parity, has):
                tally.next(q_stacked, 16 * 12)
                tally.next(m_stacked, 16)
                if parity == 0:
                    tally.add(v_ready)
                for slot in range(3 * NQUAD):
                    quad, r = slot // 3, slot % 3
                    if r == 0 and parity == 0:
                        tally.next(ks_in[quad], 16 * 6)
                    k = 4 * (slot - 2) if has["prepare"] and 2 <= slot < 8 else None
                    scores(quad, 2 * r, parity)
                    if k is not None:
                        scores_for_maxima(k, k + 1)
                    scores(quad, 2 * r + 1, parity)
                    if k is not None:
                        scores_for_maxima(k + 1, k + 2)
                    if has["prepare"]:
                        if slot == 0:
                            norm_turned()
                        if slot == 1:
                            queries()
                        if slot == 9:
                            maxima()
                    if has["route"] and slot == 3:
                        route_turned()
                    if has["finish"] and 4 <= slot < 4 + TPC:
                        outputs_turned(slot - 4, 1 - parity)
                    if has["route"] and slot == 8:
                        router_logits()
                    if parity == 0 and has["load"]:
                        if slot == 10:
                            project_keys()
                        if slot == 11:
                            project_values()
                    if k is not None:
                        scores_for_maxima(k + 2, k + 3)
                    if slot == 3 and parity == 0:
                        tally.wait(v_ready, tally.n["v_ready"])
                    if quad > 0 or has["finish"]:
                        weighted((quad - 1) % NQUAD, r)
                    if k is not None:
                        scores_for_maxima(k + 3, k + 4)

            every_chunk(tally, chunk)
            for r in range(3):
                weighted(NQUAD - 1, r)
            for t in range(TPC):
                outputs_turned(t, 1)
            for g in (NCH - 2, NCH - 1):
                route_turned()
                router_logits()

            attention_over(pe)
            for k in range(NCH):
                pe.wait_ge(copies_ready, NCH)
                for t in range(TPC):
                    last = pe.transpose(bank[k][:, t * P:(t + 1) * P], copies[:, k * TPC + t, :],
                                        ident)
                last.then_inc(copies_turned, 1)
            pe.wait_ge(scoresT_ready, NCH)
            for r in range(ROUNDS):
                pe.wait_ge(feasible, r + 1)
                pe.matmul(bank[r % 2][:, 0:1], cf[:, C_BLOCK:C_BLOCK + P], count[:, 1:2], start=True,
                          stop=True).then_inc(counted, 1)
            pe.wait_ge(wide_ready, 1)
            pe.transpose(bank[2][:, 0:P], wide[:, :], ident).then_inc(thr_turned, 1)

            def ranks(to, mask):
                pe.matmul(to[:, 0:NE * NT], cb[:, B_TRI:B_TRI + P],
                          mask[:, :, :].rearrange("p e t -> p (e t)"), start=True, stop=False)
                return pe.matmul(to[:, 0:NE * NT], cb[:, B_ONES:B_ONES + P],
                                 before[:, :, :].rearrange("p e t -> p (e t)"), start=False, stop=True)

            pe.wait_ge(same_ready, 1)
            pe.matmul(bank[3][:, 0:NE], cb[:, B_ONES:B_ONES + P], cum_over[:, :, NT - 1],
                      start=True, stop=True)
            ranks(bank[4], same).then_inc(same_ranked, 1)
            pe.wait_ge(taken_ready, 1)
            ranks(bank[5], taken).then_inc(taken_ranked, 1)

            SPLITS = ((0, 0), (0, 1), (1, 0))

            def list_tokens(t):
                if t == 0:
                    tally.next(values_ready)
                if t % (NT // HOTS) == 0:
                    tally.next(hot_ready)
                last = pe.matmul(LISTB[:, 0:ST * 5], hot_lo[:, t, :],
                                 values[:, t, :, :].rearrange("p k v -> p (k v)"),
                                 start=(t == 0), stop=(t == NT - 1))
                if t == NT - 1:
                    last.then_inc(list_full, 1)

            def turn_x(g):
                h, d = g // KD, g % KD
                if d == 0:
                    tally.next(gathered[h], 8 * ST)
                tally.wait(xlo_ready, tally.add(xlo_ready) - 2)
                for t in range(TPC):
                    last = pe.transpose(TURNB[g % 2][:, t * P:(t + 1) * P],
                                        xg[:, h * TPC + t, d * P:(d + 1) * P], ident)
                last.then_inc(x_turned, 1)

            def expert(e, has_next):
                for k in range(2 * MT):
                    h, m = k // MT, k % MT
                    if k == 0:
                        tally.next(w1hi_ready, PIECES)
                        tally.next(w1lo_ready, PIECES)
                        tally.wait(xlo_ready, tally.n["xlo_ready"] - 2)
                    if k == 3:
                        tally.wait(xlo_ready, tally.n["xlo_ready"])
                    tally.wait(gelu_done, tally.add(gelu_done) - 4)
                    for i, (a, b) in enumerate(SPLITS):
                        for d in range(KD):
                            at = d * DI + m * P
                            last = pe.matmul(HIDB[k % 4][:, :], w1s[a][:, at:at + P],
                                             xt[b][:, d, h * CT:(h + 1) * CT],
                                             start=(i == 0 and d == 0), stop=(i == 2 and d == KD - 1))
                            if i == 2 and d == KD - 1:
                                last.then_inc(hidden_full, 1)
                            t = (k - LISTS_AT) * 6 + i * KD + d
                            if has_next and 0 <= t < NT:
                                list_tokens(t)
                for n in range(ST):
                    if n == 0:
                        tally.next(w2hi_ready, PIECES)
                        tally.next(w2lo_ready, PIECES)
                    if n % TPC == 0:
                        tally.next(hid_ready, MT)
                    tally.wait(y_taken, tally.add(y_taken) - 2)
                    for m in range(MT):
                        for i, (a, b) in enumerate(SPLITS):
                            last = pe.matmul(YB[n % 2][:, 0:D], hid[a][:, m, n * P:(n + 1) * P],
                                             w2s[b][:, m * D:(m + 1) * D],
                                             start=(m == 0 and i == 0), stop=(m == MT - 1 and i == 2))
                    last.then_inc(y_full, 1)
                    if has_next and 3 <= n < 7:
                        turn_x(n - 3)

            for t in range(NT):
                list_tokens(t)
            for g in range(4):
                turn_x(g)
            every_expert(tally, expert)

        @block.vector
        def _(dve):
            tally = Tally(dve, per_batch)

            def step(ins):
                ins.then_inc(dve_step, 1)
                tally.add(dve_step)

            def settle():
                tally.wait(dve_step, tally.n["dve_step"])

            def so_far(*events):
                for s in events:
                    tally.wait(s, tally.n.get(s.name, 0))

            def statistics(k, src, done):
                for t in range(TPC):
                    step(dve.bn_stats(bn[:, k, t, :], src[:, t, :]))
                settle()
                dve.memset(idle[:, :], 0.0)
                for t in range(TPC):
                    last = dve.bn_aggr(mv[:, k, t, :], bn[:, k, t, :])
                last.then_inc(done, 1)
                tally.add(done)

            def normalise(k, to, src, rstd_sem, done):
                tally.next(rstd_sem)
                for t in range(TPC):
                    last = dve.tensor_scalar(to[:, t, :], src[:, t, :], mv[:, k, t, 0:1],
                                             rstd[:, k, t:t + 1], ALU.subtract, ALU.mult)
                last.then_inc(done, 1)
                tally.add(done)

            def first_statistics(parity):
                tally.next(xc_in[parity], 16)
                statistics(0, xc[:, parity], ln1_stats)

            def first_norm(parity):
                so_far(xnT_ready)
                normalise(0, xn, xc[:, parity], ln1_rstd, xn_ready)
                tally.add(xnT_ready, KD)

            def keys():
                tally.next(khi_ready, KD)
                for et in range(KD):
                    dve.scalar_tensor_tensor(klo[:, et, :], MISC[0][:, et * 256:et * 256 + L2],
                                             bk[:, et:et + 1], khi[:, et, :].bitcast(f32),
                                             ALU.add, ALU.subtract).then_inc(klo_ready, 1)
                    tally.add(klo_ready)

            def stage_keys():
                tally.wait(klo_ready, tally.n["klo_ready"])
                for j in range(HPT):
                    last = dve.tensor_scalar(kbd[:, :, j, :], khi[:, :, :].bitcast(f32),
                                             cf[:, C_HEAD + j:C_HEAD + j + 1], None, ALU.mult)
                last.then_inc(kbd_ready, 1)
                so_far(*ks_in)
                for part, src in enumerate((khi, klo)):
                    for s in range(2):
                        own = cf[:, C_HALF + s:C_HALF + s + 1]
                        dve.tensor_scalar(kst[part][:, :, s * P:(s + 1) * P],
                                          src[:, :, 0:P].bitcast(f32), own, None, ALU.mult)
                        for at in (0, 32):
                            a = 2 * P + 64 * s + at
                            last = dve.tensor_scalar(kst[part][:, :, a:a + REM],
                                                     src[:, :, P:L2].bitcast(f32), own, None,
                                                     ALU.mult)
                last.then_inc(kst_ready, 1)
                for s in ks_in:
                    tally.add(s, 16 * 6)

            def values():
                tally.next(v_staged)
                so_far(av_done)
                bvh = bv[:, :].rearrange("p (h d) -> p h d", d=DH)
                vs = [vst[:, i, :].rearrange("p (h d) -> p h d", d=DH) for i in range(2)]
                dve.tensor_tensor(vmain[:, :, 0:DH], vs[0], bvh, ALU.add)
                for s in range(2):
                    rows = slice(64 * s, 64 * s + REM)
                    last = dve.tensor_tensor(vrem[rows, s::2, 0:DH], vs[1][rows, s::2, :],
                                             bvh[rows, s::2, :], ALU.add)
                last.then_inc(v_ready, 1)

            def queries():
                so_far(q_stacked)
                for et in range(KD):
                    tally.next(qhi_ready)
                    dve.scalar_tensor_tensor(qlo[:, et, :], MISC[et][:, :], bq[:, et:et + 1],
                                             qhi[:, et, :].bitcast(f32), ALU.add, ALU.subtract)\
                       .then_inc(qlo_ready, 1)
                tally.add(q_stacked, 16 * 12)

            def maxima(place_values=False):
                k = 0
                for t in range(TPC):
                    for et in range(KD):
                        for j, n in MAX_GROUPS:
                            tally.next(max_full)
                            dve.tensor_reduce(maxes[:, t, et * HPT + j:et * HPT + j + n],
                                              MAXB[k % 2][:, 0:n * L2]
                                              .rearrange("p (j n) -> p j n", n=L2), AX, ALU.max)\
                               .then_inc(max_free, 1)
                            tally.add(max_free)
                            k += 1
                            if place_values and k == 4:
                                values()
                so_far(max_free, negmaxT_ready)
                step(dve.tensor_scalar(negmax[:, :, 0, :], maxes[:, :, :], -1.0, None, ALU.mult))
                settle()
                dve.scalar_tensor_tensor(negmax[:, :, 1, :], maxes[:, :, :], -1.0,
                                         negmax[:, :, 0, :].bitcast(f32), ALU.mult,
                                         ALU.subtract).then_inc(negmax_ready, 1)
                tally.add(negmaxT_ready)

            def rescale():
                tally.next(ot_ready, TPC)
                so_far(res_ready)
                ss = ot[:, :, DH]
                step(dve.tensor_scalar(ri[:, :], ss.bitcast(i32), 1, None, ALU.logical_shift_right))
                settle()
                step(dve.tensor_scalar(rs[:, :].bitcast(i32), ri[:, :], -1.0, float(RSQRT_SEED),
                                       ALU.mult, ALU.add))
                settle()
                for n in range(3):
                    step(dve.scalar_tensor_tensor(rt[:, :], rs[:, :], -0.5, rs[:, :], ALU.mult,
                                                  ALU.mult))
                    settle()
                    step(dve.tensor_tensor(rt[:, :], rt[:, :], ss, ALU.mult))
                    settle()
                    last = dve.scalar_tensor_tensor(rs[:, :], rt[:, :], 1.5, rs[:, :], ALU.add,
                                                    ALU.mult)
                    if n < 2:
                        step(last)
                        settle()
                last.then_inc(rs_ready, 1)
                tally.add(res_ready)

            def residual():
                so_far(res_ready, x1_stored)
                tally.next(xr_in, 16)
                dve.tensor_tensor(x1[:, :, :].rearrange("p t d -> p (t d)"),
                                  res[:, :, :].rearrange("p h d -> p (h d)"),
                                  xr[:, :, :].rearrange("p t d -> p (t d)"), ALU.add)\
                   .then_inc(x1_ready, 1)
                tally.add(x1_ready)
                tally.add(x1_stored, 16)
                so_far(x1_ready)
                statistics(1, x1, ln2_stats)

            def second_norm():
                so_far(x2n_stored, x2T_ready)
                normalise(1, x2n, x1, ln2_rstd, x2n_ready)
                tally.add(x2n_stored, 16)
                tally.add(x2T_ready, KD)

            dve.memset(vmain[:, :, :].rearrange("p h r -> p (h r)"), 0.0)
            dve.wait_ge(first_in, 16 * FIRST_LOADS)
            dve.tensor_copy(vrem[:, :, :].rearrange("p h r -> p (h r)"), cf[:, C_VR:C_VR + H * 32])\
               .then_inc(vrem_const, 1)
            dve.wait_ge(vrem_const, 1)
            dve.wait_ge(kst_clear, 1)
            first_statistics(0)
            first_norm(0)
            keys()
            stage_keys()
            values()
            queries()
            maxima()
            first_statistics(1)
            first_norm(1)

            def chunk(b, g, parity, has):
                if has["route"]:
                    second_norm()
                if has["prepare"]:
                    queries()
                if has["finish"]:
                    tally.add(av_done, NQUAD)
                if has["prepare"]:
                    maxima(place_values=(parity == 0 and has["finish"]))
                if has["load"]:
                    first_statistics(parity)
                if has["finish"]:
                    rescale()
                if has["load"]:
                    first_norm(parity)
                    if parity == 0:
                        keys()
                if has["finish"]:
                    residual()
                if has["load"] and parity == 0:
                    stage_keys()

            every_chunk(tally, chunk)
            second_norm()
            rescale()
            residual()
            second_norm()

            attention_over(dve)
            settle()
            over_t = [P, NE, NT]
            turned = logits[:, :, :].rearrange("p t e -> p e t")
            step(dve.tensor_reduce(best[:, 0, :], logits[:, :, :], AX, ALU.max))
            settle()
            dve.tensor_tensor(scores[:, :, :], turned,
                              best[:, 0:1, :].broadcast_to(over_t), ALU.subtract)\
               .then_inc(maxima_taken, 1)
            dve.wait_ge(exps_ready, 1)
            step(dve.tensor_reduce(best[:, 1, :], exps[:, :, :].rearrange("p e t -> p t e"), AX,
                                   ALU.add))
            settle()
            step(dve.reciprocal(best[:, 2, :], best[:, 1, :]))
            settle()
            dve.tensor_tensor(scores[:, :, :], exps[:, :, :],
                              best[:, 2:3, :].broadcast_to(over_t), ALU.mult)\
               .then_inc(scores_ready, 1)
            dve.wait_ge(scores_ready, 1)
            for k in range(0, NCH, 2):
                dve.tensor_copy(copies[:, k * TPC:(k + 1) * TPC, :]
                                .rearrange("p t (e j) -> p t e j", e=NE),
                                scores[:, :, k * TPC:(k + 1) * TPC].rearrange("p e (t a) -> p t e a", a=1)
                                .broadcast_to([P, TPC, NE, P // NE])).then_inc(copies_ready, 1)
            dve.memset(found[:, :], 0)
            for k in range(0, NCH, 2):
                dve.wait_ge(copies_turned, k + 1)
                dve.tensor_copy(scoresT[:, k * CT:(k + 1) * CT], bank[k][:, :])\
                   .then_inc(scoresT_ready, 1)
            dve.wait_ge(scoresT_ready, NCH)

            def low_w(i, raw, parts, hi_ready, lo_ready):
                n = raw.shape[1] // PIECES
                tally.next(hi_ready)
                cols = slice(i * n, (i + 1) * n)
                dve.tensor_tensor(parts[1][:, cols], raw[:, cols], parts[0][:, cols].bitcast(f32),
                                  ALU.subtract).then_inc(lo_ready, 1)

            for r in range(ROUNDS):
                grain = float(1 << SHIFTS[r])
                step(dve.tensor_tensor(found[:, 1:2], found[:, 0:1], ci[:, r:r + 1], ALU.bitwise_or))
                settle()
                step(dve.tensor_scalar(above[:, :], scoresT[:, :], found[:, 1:2].bitcast(f32), 0.0,
                                       ALU.is_ge, ALU.add, accum_out=count[:, 0:1]))
                settle()
                dve.tensor_scalar(count[:, 1:2], count[:, 0:1], float(CAP), None, ALU.is_ge)\
                   .then_inc(feasible, 1)
                low_w(r, w1raw, w1s, w1hi_ready, w1lo_ready)
                dve.wait_ge(counted, r + 1)
                times = 1.0 if SHIFTS[r] else 0.25
                step(dve.tensor_scalar(found[:, 2:3], bank[r % 2][:, 0:1], grain * times, -grain,
                                       ALU.mult, ALU.add))
                settle()
                step(dve.tensor_tensor(found[:, 0:1], found[:, 0:1], found[:, 2:3], ALU.bitwise_or))
                settle()

            dve.tensor_copy(wide[:, :], found[:, 0:1].bitcast(f32).broadcast_to([P, P]))\
               .then_inc(wide_ready, 1)
            dve.wait_ge(thr_turned, 1)
            step(dve.tensor_copy(thr[:, :], bank[2][:, 0:P:P // NE]))
            settle()
            at_thr = thr[:, :].rearrange("p (e a) -> p e a", a=1).broadcast_to(over_t)
            flat = "p e t -> p (e t)"

            def running(to, mask):
                return dve.tensor_tensor_scan(to[:, :, :].rearrange(flat), fresh[:, :],
                                              mask[:, :, :].rearrange(flat), 0.0, ALU.mult, ALU.add)

            dve.tensor_tensor(over[:, :, :], scores[:, :, :], at_thr, ALU.is_gt)
            step(dve.tensor_tensor(same[:, :, :], scores[:, :, :], at_thr, ALU.is_equal))
            settle()
            dve.wait_ge(fresh_ready, 1)
            running(cum_over, over)
            step(running(cum, same))
            settle()
            dve.tensor_tensor(before[:, :, :], cum[:, :, :], same[:, :, :], ALU.subtract)\
               .then_inc(same_ready, 1)
            dve.wait_ge(same_ranked, 1)
            step(dve.tensor_scalar(need[:, :], bank[3][:, 0:NE], -1.0, float(CAP), ALU.mult, ALU.add))
            settle()
            step(dve.tensor_tensor(taken[:, :, :], bank[4][:, 0:NE * NT].rearrange("p (e t) -> p e t", e=NE),
                                   need[:, :].rearrange("p (e a) -> p e a", a=1).broadcast_to(over_t),
                                   ALU.is_lt))
            settle()
            step(dve.tensor_tensor(taken[:, :, :], taken[:, :, :], same[:, :, :], ALU.mult))
            settle()
            step(dve.tensor_tensor(taken[:, :, :], taken[:, :, :], over[:, :, :], ALU.add))
            settle()
            step(running(cum, taken))
            settle()
            dve.tensor_tensor(before[:, :, :], cum[:, :, :], taken[:, :, :], ALU.subtract)\
               .then_inc(taken_ready, 1)
            dve.wait_ge(taken_ranked, 1)
            step(dve.tensor_copy(slot[:, 0, :, :].rearrange(flat), bank[5][:, 0:NE * NT]))
            settle()
            dve.tensor_scalar(slot[:, 1, :, :], slot[:, 0, :, :], P - 1, None, ALU.bitwise_and)
            dve.tensor_scalar(slot[:, 2, :, :], slot[:, 0, :, :], 7, None, ALU.logical_shift_right)
            step(dve.tensor_scalar(exps[:, :, :], taken[:, :, :], -1000.0, 1000.0, ALU.mult, ALU.add))
            settle()
            dve.tensor_copy(slot_hi[:, :, :], slot[:, 2, :, :])
            step(dve.tensor_copy(slot_lo[:, :, :], slot[:, 1, :, :]))
            settle()
            dve.tensor_tensor(slot_lo[:, :, :], slot_lo[:, :, :], exps[:, :, :], ALU.add)\
               .then_inc(slots_ready, 1)
            dve.wait_ge(slots_ready, 1)

            def hot_slots(e, i):
                n = NT // HOTS
                dve.tensor_tensor(hot_lo[:, i * n:(i + 1) * n, :],
                                  cb[:, B_IOTA:B_IOTA + P].rearrange("p (a k) -> p a k", a=1)
                                  .broadcast_to([P, n, P]),
                                  slot_lo[:, e, i * n:(i + 1) * n].rearrange("p (t a) -> p t a", a=1)
                                  .broadcast_to([P, n, P]), ALU.is_equal).then_inc(hot_ready, 1)

            def high_slots(e):
                so_far(values_ready)
                dve.tensor_tensor(hot_hi[:, :, :],
                                  cb[:, B_IOTA8:B_IOTA8 + ST].rearrange("p (a k) -> p a k", a=1)
                                  .broadcast_to([P, NT, ST]),
                                  slot_hi[:, e, :].rearrange("p (t a) -> p t a", a=1)
                                  .broadcast_to([P, NT, ST]), ALU.is_equal).then_inc(hot_hi_ready, 1)
                tally.add(values_ready)

            def take_list():
                tally.next(list_full)
                step(dve.tensor_copy(packed[:, :, :].rearrange("p k v -> p (k v)"),
                                     LISTB[:, 0:ST * 5]))
                settle()
                so_far(*gathered)
                step(dve.tensor_tensor(gate_next[:, :], packed[:, :, 3], packed[:, :, 4], ALU.add))
                settle()
                dve.tensor_tensor(gate_next[:, :], gate_next[:, :], packed[:, :, 2], ALU.add)
                dve.scalar_tensor_tensor(tok_next[:, :], packed[:, :, 1], float(P), packed[:, :, 0],
                                         ALU.mult, ALU.add).then_inc(list_ready, 1)
                tally.add(list_ready)
                for s in gathered:
                    tally.add(s, 8 * ST)

            def keep_list():
                so_far(list_ready)
                so_far(scattered)
                dve.tensor_copy(tok_now[:, :], tok_next[:, :])
                step(dve.tensor_copy(gate_now[:, :], gate_next[:, :]))
                settle()
                tally.add(scattered, 16 * ST)

            def take_bias(e):
                dve.tensor_copy(b1c[:, :], b1[:, e, :]).then_inc(b1c_ready, 1)

            def low_x(g):
                h, d = g // KD, g % KD
                tally.next(xhi_ready)
                cols = slice(h * CT, (h + 1) * CT)
                dve.tensor_tensor(xt[1][:, d, cols], TURNB[g % 2][:, :],
                                  xt[0][:, d, cols].bitcast(f32), ALU.subtract).then_inc(xlo_ready, 1)

            def expert(e, has_next):
                for k in range(2 * MT):
                    h, m = k // MT, k % MT
                    cols = slice(h * CT, (h + 1) * CT)
                    tally.next(gelu_done)
                    step(dve.tensor_copy(hid[0][:, m, cols], hact[:, k % 4, :]))
                    if has_next and k == 0:
                        high_slots(e + 1)
                    if has_next and k < HOTS:
                        hot_slots(e + 1, k)
                    if 4 <= k < 4 + PIECES:
                        low_w(k - 4, w2raw, w2s, w2hi_ready, w2lo_ready)
                    settle()
                    dve.tensor_tensor(hid[1][:, m, cols], hact[:, k % 4, :],
                                      hid[0][:, m, cols].bitcast(f32), ALU.subtract)\
                       .then_inc(hid_ready, 1)
                    if k == 7:
                        keep_list()
                    if has_next and k == LISTS_AT + 6:
                        take_list()
                if has_next:
                    take_bias(e + 1)
                for n in range(ST):
                    if n == 0:
                        tally.next(b2_in, 16)
                    tally.next(y_full)
                    dve.tensor_tensor(y[:, n, :], YB[n % 2][:, 0:D], b2c[:, :], ALU.add)\
                       .then_inc(y_taken, 1)
                    if has_next and n < PIECES // 2:
                        for i in (2 * n, 2 * n + 1):
                            low_w(i, w1raw, w1s, w1hi_ready, w1lo_ready)
                    tally.next(y_taken)
                    dve.tensor_scalar(y[:, n, :], y[:, n, :], gate_now[:, n:n + 1], None, ALU.mult)\
                       .then_inc(y_ready, 1)
                    if has_next and 3 <= n < 7:
                        low_x(n - 3)

            high_slots(0)
            for i in range(HOTS):
                hot_slots(0, i)
            take_bias(0)
            take_list()
            for g in range(4):
                low_x(g)
            every_expert(tally, expert)

        @block.gpsimd
        def _(pool):
            tally = Tally(pool, per_batch)

            def so_far(*events):
                for s in events:
                    tally.wait(s, tally.n.get(s.name, 0))

            def deviations(k, stats, done):
                tally.next(stats)
                pool.tensor_tensor(veps[:, k, :], mv[:, k, :, 1], eps[:, :], ALU.add)\
                    .then_inc(pool_step, 1)
                tally.next(pool_step)
                pool.tensor_tensor(rstd[:, k, :], veps[:, k, :], minus_half[:, :], ALU.pow)\
                    .then_inc(done, 1)

            def squares(quad, between=None):
                tally.wait(av_done, tally.add("quads") - 2)
                base = tally.n.get("exp_done", 0)
                for i in range(2):
                    for part in range(2):
                        n = TILES.index((i, part))
                        tally.wait(exp_done, base + n + 1)
                        e = ex[:, (quad % 2) * 6 + n, :]
                        pool.tensor_tensor(sq[:, (quad % 2) * 4 + 2 * i + part, :], e, e, ALU.mult)\
                            .then_inc(sq_done, 1)
                        if between and (i, part) == (0, 1):
                            between()
                tally.add(exp_done, 6)

            def rescaled():
                tally.next(rs_ready)
                so_far(x1_ready)
                pool.tensor_tensor(res[:, :, :], ot[:, :, 0:DH],
                                   rs[:, :].rearrange("p (h a) -> p h a", a=1)
                                   .broadcast_to([P, TPC * H, DH]), ALU.mult).then_inc(res_ready, 1)
                tally.add(x1_ready)

            pool.memset(minus_half[:, :], -0.5)
            pool.memset(eps[:, :], EPS)
            for part in range(2):
                last = pool.memset(kst[part][:, :, :].bitcast(f32), 0.0)
            last.then_inc(kst_clear, 1)
            pool.wait_ge(kst_clear, 1)
            pool.wait_ge(ks_const, 1)
            deviations(0, ln1_stats, ln1_rstd)
            deviations(0, ln1_stats, ln1_rstd)

            def chunk(b, g, parity, has):
                for quad in range(NQUAD - 1):
                    squares(quad)
                if has["load"]:
                    deviations(0, ln1_stats, ln1_rstd)
                squares(NQUAD - 1, between=rescaled if has["finish"] else None)
                if has["finish"]:
                    deviations(1, ln2_stats, ln2_rstd)

            every_chunk(tally, chunk)
            rescaled()
            deviations(1, ln2_stats, ln2_rstd)

            attention_over(pool)
            pool.memset(fresh[:, :].rearrange("p (e t) -> p e t", e=NE)[:, :, 1:NT], 1.0)
            pool.memset(fresh[:, 0:NE * NT:NT], 0.0).then_inc(fresh_ready, 1)
            pool.memset(carrier[:, 0:1], 0.0)
            pool.wait_ge(scores_ready, 1)
            rest = scores
            for i in range(3):
                pool.tensor_copy(gate3[:, :, :, i], rest[:, :, :]).then_inc(gates_split, 1)
                pool.wait_ge(gates_split, 2 * i + 1)
                if i < 2:
                    pool.tensor_tensor(gate_rest[:, :, :], rest[:, :, :], gate3[:, :, :, i],
                                       ALU.subtract).then_inc(gates_split, 1)
                    pool.wait_ge(gates_split, 2 * i + 2)
                rest = gate_rest

            def list_values(e):
                so_far(list_full)
                tally.next(hot_hi_ready)
                for first, n, src in ((0, 2, cb[:, B_TOK:B_TOK + 2 * NT]
                                       .rearrange("p (t a v) -> p t a v", a=1, v=2)),
                                      (2, 3, gate3[:, e, :, :].rearrange("p t (a v) -> p t a v", a=1))):
                    last = pool.tensor_tensor(values[:, :, :, first:first + n],
                                              hot_hi[:, :, :].rearrange("p t (k a) -> p t k a", a=1)
                                              .broadcast_to([P, NT, ST, n]),
                                              src.broadcast_to([P, NT, ST, n]), ALU.mult)
                last.then_inc(values_ready, 1)
                tally.add(list_full)

            def carry():
                so_far(carried)
                pool.tensor_tensor(carrier[:, 1:2], carrier[:, 0:1], carrier[:, 0:1], ALU.mult)\
                    .then_inc(carried, 1)
                tally.add(carried)

            def gather():
                tally.next(list_ready)
                so_far(x_turned)
                carry()
                for n in range(ST):
                    pool.indirect_dma_start(xg[:, n, :], None, x2n_rows[:, :],
                                            bass.IndirectOffsetOnAxis(tok_next[:, n:n + 1], axis=0))\
                        .then_inc(gathered[n // TPC], 16)
                tally.add(x_turned, 4)

            def scatter():
                for n in range(ST):
                    tally.next(y_ready)
                    carry()
                    pool.indirect_dma_start(out_d[:, :],
                                            bass.IndirectOffsetOnAxis(tok_now[:, n:n + 1], axis=0),
                                            y[:, n, :], None, compute_op=ALU.add)\
                        .then_inc(scattered, 16)

            def expert(e, has_next):
                if has_next:
                    list_values(e + 1)
                    gather()
                scatter()

            pool.wait_ge(slots_ready, 1)
            list_values(0)
            gather()
            every_expert(tally, expert)


def kernel(x, ctx_1024, L0_xattn_Wq, L0_xattn_bq, L0_xattn_Wk, L0_xattn_bk, L0_xattn_Wv, L0_xattn_bv,
           L0_ffn_Wr, L0_ffn_W1, L0_ffn_b1, L0_ffn_W2, L0_ffn_b2):
    import numpy as _np
    import concourse.bacc as _bacc
    from concourse import mybir as _mybir
    from concourse.bass_utils import run_bass_kernel_spmd as _run

    def array(a):
        return _np.ascontiguousarray(_np.asarray(a))

    context = array(ctx_1024).transpose(0, 2, 1)
    columns = _np.zeros((B, D, L2 + P), context.dtype)
    columns[:, :, :L2] = context
    columns[:, :, L2:L2 + REM] = context[:, :, P:]
    columns[:, :, L2 + 64:L2 + 64 + REM] = context[:, :, P:]
    cf, cb, ci, ck = constants()
    arrays = {
        "x": array(x).reshape(N, D),
        "ctx": columns,
        "wq": array(array(L0_xattn_Wq).T), "wk": array(array(L0_xattn_Wk).T),
        "wv": array(array(L0_xattn_Wv).T),
        "bq": array(array(L0_xattn_bq).reshape(KD, P).T),
        "bk": array(array(L0_xattn_bk).reshape(KD, P).T),
        "bv": array(L0_xattn_bv),
        "wr": array(L0_ffn_Wr),
        "w1": array(L0_ffn_W1),
        "b1": array(array(L0_ffn_b1).reshape(NE, MT, P).transpose(2, 0, 1)),
        "w2": array(L0_ffn_W2), "b2": array(L0_ffn_b2),
        "cf": cf, "cb": cb, "ci": ci, "ck": ck,
    }
    nc = _bacc.Bacc("TRN2", target_bir_lowering=False, num_devices=1)
    args = [nc.dram_tensor(f"{k}_dram", a.shape, _mybir.dt.from_np(a.dtype), kind="ExternalInput").ap()
            for k, a in arrays.items()]
    out = nc.dram_tensor("out_dram", (N, D), _mybir.dt.float32, kind="ExternalOutput").ap()
    build_kernel(nc, *args, out)
    r = _run(nc, [{f"{k}_dram": a for k, a in arrays.items()}], core_ids=[0])
    return r.results[0]["out_dram"].reshape(B, L1, D)
```

```python
import numpy as np
import concourse.bass as bass
from concourse import mybir
from contextlib import ExitStack

B, L1, L2, D = 4, 1024, 154, 256
H, DH = 16, 16
NE, DI, CAP = 8, 1024, 1024
P = 128
N = B * L1
CT = 512
TPC = CT // P
NCH = N // CT
NT = N // P
KD = D // P
REM = L2 - P
HPT = P // DH
NPAIR = H // 2
NQUAD = H // 4
MT = DI // P
ST = CAP // P
EPS = 1e-5
SCALE = 1.0 / DH ** 0.5
RSQRT_SEED = 0x5F3759DF
FIRST_LOADS, LATE_LOADS = 6, 5
EXPERT_STEPS = 19
PIECES = 8
LISTS_AT = 6
HOTS = 4
PRIMED = {"logits_ready": 1, "x2T_ready": 1, "x2n_stored": 16}
DVE_STEPS = 38
SHIFTS = [10, 6, 2, 0] + [12, 8, 4, 0]
ROUNDS, HALF = len(SHIFTS), 4
SCAN = 2560
MAX_GROUPS = [(0, 3), (3, 3), (6, 2)]

C_IDENT = 0
C_HALF = C_IDENT + P
C_HEAD = C_HALF + 2
C_ESC = C_HEAD + HPT
C_SUM = C_ESC + 1
C_VR = C_SUM + 32
C_CAND = C_VR + H * 32
C_BLOCK = C_CAND + ROUNDS
C_ALL = C_BLOCK + P
B_TRI, B_ONES, B_IOTA, B_TOK = 0, 128, 256, 384
B_IOTA8 = B_TOK + NT * 2
B_ALL = B_IOTA8 + ST


def constants():
    p = np.arange(P)
    c = np.zeros((P, C_ALL), np.float32)
    c[:, C_IDENT:C_IDENT + P] = np.eye(P)
    c[:, C_BLOCK:C_BLOCK + P] = p[:, None] // 16 == p[None] // 16
    for s in range(2):
        c[:, C_HALF + s] = (p % 32) // 16 == s
    for j in range(HPT):
        c[:, C_HEAD + j] = p // DH == j
    c[:, C_ESC] = np.where((p // 32) % 2 == 0, SCALE, 2 * SCALE)
    c[:, C_SUM + DH] = 1
    vr = np.zeros((P, H, 32), np.float32)
    vr[32:32 + REM, 0::2, DH] = 1
    vr[96:96 + REM, 1::2, DH] = 1
    c[:, C_VR:C_VR + H * 32] = vr.reshape(P, -1)
    ks = np.zeros((P, NPAIR, 3 * P), np.float32)
    for h in range(H):
        i, s = h // 2, h % 2
        for row in (96 + h, 112 + h):
            ks[row, i, s * P:(s + 1) * P] = 1
            for at in (0, 32):
                ks[row, i, 2 * P + 64 * s + at:2 * P + 64 * s + at + REM] = 1
    b = np.zeros((P, B_ALL), np.float32)
    b[:, B_TRI:B_TRI + P] = p[:, None] < p[None]
    b[:, B_ONES:B_ONES + P] = 1
    b[:, B_IOTA:B_IOTA + P] = p[None]
    b[:, B_TOK:B_TOK + 2 * NT:2] = p[:, None]
    b[:, B_TOK + 1:B_TOK + 2 * NT:2] = np.arange(NT)[None]
    b[:, B_IOTA8:] = np.arange(ST)[None]
    j = p % 16
    for r, s in enumerate(SHIFTS):
        c[:, C_CAND + r] = (j & 3) if r == HALF - 1 else j << s
    return c, b, ks[96:].reshape(32, -1)


class Tally:

    def __init__(self, engine, per_batch):
        self.engine, self.per_batch, self.trip = engine, per_batch, None
        self.n = dict(PRIMED)

    def add(self, sem, k=1):
        name = sem if isinstance(sem, str) else sem.name
        self.n[name] = self.n.get(name, 0) + k
        return self.n[name]

    def wait(self, sem, value):
        if self.trip is not None:
            assert value > 0, sem.name
            self.engine.wait_ge(sem, self.trip * self.per_batch[sem.name] + value)
        elif value > 0:
            self.engine.wait_ge(sem, value)

    def next(self, sem, k=1):
        self.wait(sem, self.add(sem, k))

    def loop(self, first, end, body):
        before = dict(self.n)
        with self.engine.Fori(0, end - first) as trip:
            self.trip = trip
            body(trip + first)
            self.trip = None
        for name, n in self.n.items():
            d = n - before.get(name, 0)
            assert d == 0 or d == self.per_batch[name], (name, d, self.per_batch[name])
            self.n[name] = n + d * (end - first - 1)


def build_kernel(nc, x_d, ctx_d, wq_d, wk_d, wv_d, bq_d, bk_d, bv_d, wr_d, w1_d, b1_d, w2_d, b2_d,
                 cf_d, cb_d, ck_d, out_d):
    f32, f32r, bf16 = mybir.dt.float32, mybir.dt.float32r, mybir.dt.bfloat16
    i32, u32, u16 = mybir.dt.int32, mybir.dt.uint32, mybir.dt.uint16
    ALU, ACT, AX = mybir.AluOpType, mybir.ActivationFunctionType, mybir.AxisListType.X
    ctx = ExitStack()
    with ctx:
        def sb(name, shape, dt, stack=ctx):
            return stack.enter_context(nc.sbuf_tensor(name, shape, dt))

        sems = {}

        def sem(name):
            sems[name] = ctx.enter_context(nc.semaphore(name))
            return sems[name]

        x2n_rows = nc.dram_tensor("x2n_rows", [N, D], f32, kind="Internal").ap()
        x_c = x_d.rearrange("(g t p) d -> g p t d", t=TPC, p=P)
        out_c = out_d.rearrange("(g t p) d -> g p t d", t=TPC, p=P)
        x2n_c = x2n_rows.rearrange("(g t p) d -> g p t d", t=TPC, p=P)

        cf = sb("cf", [P, C_ALL], f32)
        cb = sb("cb", [P, B_ALL], bf16)
        ident = cf[:, C_IDENT:C_IDENT + P]
        wr = sb("wr", [P, KD, 32], f32)
        b1 = sb("b1", [P, NE, MT], f32)
        logits = sb("logits", [P, NT, NE], f32)

        att = ExitStack()
        wq = sb("wq", [P, KD, D], f32, att)
        wk = sb("wk", [P, KD, D], f32, att)
        wv = sb("wv", [P, KD, D], f32, att)
        bq = sb("bq", [P, KD], f32, att)
        bk = sb("bk", [P, KD], f32, att)
        bv = sb("bv", [P, D], f32, att)
        idle = sb("idle", [P, 1], f32, att)
        eps = sb("eps", [P, TPC], f32, att)
        minus_half = sb("minus_half", [P, TPC], f32, att)
        ctxT = sb("ctxT", [P, KD, L2 + P], f32, att)
        xc = sb("xc", [P, 2, TPC, D], f32, att)
        xr = sb("xr", [P, TPC, D], f32, att)
        xn = sb("xn", [P, TPC, D], f32, att)
        xnT = sb("xnT", [P, KD, CT], f32, att)
        qhi = sb("qhi", [P, KD, CT], f32r, att)
        qlo = sb("qlo", [P, KD, CT], f32r, att)
        khi = sb("khi", [P, KD, L2], f32r, att)
        klo = sb("klo", [P, KD, L2], f32r, att)
        kst = [sb(f"kst{i}", [P, KD, 3 * P], f32r, att) for i in range(2)]
        kbd = sb("kbd", [P, KD, HPT, L2], f32r, att)
        qs = [sb(f"qs{i}", [P, NPAIR, CT], f32r, att) for i in range(2)]
        ks = sb("ks", [P, NPAIR, 3 * P], f32r, att)
        vst = sb("vst", [P, 2, D], f32, att)
        vmain = sb("vmain", [P, H, 32], f32, att)
        vrem = sb("vrem", [P, H, 32], f32, att)
        ex = sb("ex", [P, 12, CT], f32, att)
        sq = sb("sq", [P, 8, CT], f32, att)
        osb = sb("osb", [P, 2, NQUAD, CT], f32, att)
        maxes = sb("maxes", [P, TPC, H], f32, att)
        negmax = sb("negmax", [P, TPC, 2, H], f32r, att)
        negmaxT = sb("negmaxT", [32, CT], f32r, att)
        ot = sb("ot", [P, TPC * H, DH + 1], f32, att)
        res = sb("res", [P, TPC * H, DH], f32, att)
        x1 = sb("x1", [P, TPC, D], f32, att)
        x2n = sb("x2n", [P, TPC, D], f32, att)
        logT = sb("logT", [P, P], f32, att)
        x2T = sb("x2T", [P, KD, CT], f32, att)
        bn = sb("bn", [P, 2, TPC, 6], f32, att)
        mv = sb("mv", [P, 2, TPC, 2], f32, att)
        veps = sb("veps", [P, 2, TPC], f32, att)
        rstd = sb("rstd", [P, 2, TPC], f32, att)
        rs = sb("rs", [P, TPC * H], f32, att)
        rt = sb("rt", [P, TPC * H], f32, att)
        ri = sb("ri", [P, TPC * H], i32, att)
        att.close()

        slot_lo = sb("slot_lo", [P, NE, NT], f32)
        slot_hi = sb("slot_hi", [P, NE, NT], bf16)
        gate3 = sb("gate3", [P, NE, NT, 3], bf16)
        w1raw = sb("w1raw", [P, KD * DI], f32)
        w2raw = sb("w2raw", [P, MT * D], f32)
        w1s = [sb(f"w1s{i}", [P, KD * DI], f32r) for i in range(2)]
        b1c = sb("b1c", [P, MT], f32)
        b2c = sb("b2c", [P, D], f32)
        hot_hi = sb("hot_hi", [P, NT, ST], bf16)
        values = sb("values", [P, NT, ST, 5], bf16)
        packed = sb("packed", [P, ST, 5], f32)
        tok_next = sb("tok_next", [P, ST], u32)
        tok_now = sb("tok_now", [P, ST], u32)
        gate_next = sb("gate_next", [P, ST], f32)
        gate_now = sb("gate_now", [P, ST], f32)
        carrier = sb("carrier", [P, 2], f32)

        routing = ExitStack()
        scores = sb("scores", [P, NE, NT], f32, routing)
        highs = sb("highs", [P, N], u16, routing)
        lows = sb("lows", [P, N], u16, routing)
        tails = sb("tails", [P, N], u16, routing)
        equal = sb("equal", [P, N], u16, routing)
        greater = sb("greater", [P, N], u16, routing)
        signs = sb("signs", [P, N - SCAN], bf16, routing)
        copies = sb("copies", [P, NT, P], f32, routing)
        above = sb("above", [P, SCAN], bf16, routing)
        gate_rest = sb("gate_rest", [P, NE, NT], f32, routing)
        fresh = sb("fresh", [P, NE * NT], f32, routing)
        cum = sb("cum", [P, NE, NT], bf16, routing)
        cum_over = sb("cum_over", [P, NE, NT], bf16, routing)
        over = sb("over", [P, NE, NT], bf16, routing)
        same = sb("same", [P, NE, NT], bf16, routing)
        taken = sb("taken", [P, NE, NT], bf16, routing)
        before = sb("before", [P, NE, NT], bf16, routing)
        slot = sb("slot", [P, 3, NE, NT], i32, routing)
        exps = sb("exps", [P, NE, NT], f32, routing)
        best = sb("best", [P, 3, NT], f32, routing)
        found = sb("found", [P, 2], f32, routing)
        foundi = sb("foundi", [P, 3], i32, routing)
        tried = sb("tried", [P, 2], f32, routing)
        base = sb("base", [P, 3], f32, routing)
        count = sb("count", [P, 4], f32, routing)
        wide = sb("wide", [P, P], f32, routing)
        thr = sb("thr", [P, NE], f32, routing)
        need = sb("need", [P, NE], f32, routing)
        routing.close()

        w2s = [sb(f"w2s{i}", [P, MT * D], f32r) for i in range(2)]
        xt = [sb(f"xt{i}", [P, KD, CAP], f32r) for i in range(2)]
        hid = [sb(f"hid{i}", [P, MT, CAP], f32r) for i in range(2)]
        hact = sb("hact", [P, 4, CT], f32)
        xg = sb("xg", [P, ST, D], f32)
        y = sb("y", [P, ST, D], f32)
        hot_lo = sb("hot_lo", [P, NT, P], bf16)

        bank = [ctx.enter_context(nc.psum_tensor(f"bank{i}", [P, 512], f32)) for i in range(8)]
        MAXB, SCB, OB, MISC = bank[0:3], bank[3:5], bank[5], bank[6:8]
        MAXB_FIRST = bank[0:4]
        HIDB = [bank[i] for i in (0, 1, 2, 5)]
        YB, TURNB, LISTB = bank[3:5], bank[5:7], bank[7]

        first_in = sem("first_in")
        late_in = sem("late_in")
        ks_const_in = sem("ks_const_in")
        ks_const = sem("ks_const")
        vrem_const = sem("vrem_const")
        kst_clear = sem("kst_clear")
        xc_in = [sem("xc_in0"), sem("xc_in1")]
        xr_in = sem("xr_in")
        ctx_in = sem("ctx_in")
        ln1_stats = sem("ln1_stats")
        ln1_rstd = sem("ln1_rstd")
        xn_ready = sem("xn_ready")
        xnT_ready = sem("xnT_ready")
        misc_full = [sem("misc_full0"), sem("misc_full1")]
        khi_ready = sem("khi_ready")
        klo_ready = sem("klo_ready")
        logT_ready = sem("logT_ready")
        logits_ready = sem("logits_ready")
        kbd_ready = sem("kbd_ready")
        kst_ready = sem("kst_ready")
        ks_in = [sem(f"ks_in{i}") for i in range(NQUAD)]
        v_staged = sem("v_staged")
        v_ready = sem("v_ready")
        qhi_ready = sem("qhi_ready")
        qlo_ready = sem("qlo_ready")
        q_stacked = sem("q_stacked")
        max_full = sem("max_full")
        max_free = sem("max_free")
        negmax_ready = sem("negmax_ready")
        negmaxT_ready = sem("negmaxT_ready")
        m_stacked = [sem("m_stacked0"), sem("m_stacked1")]
        score_full = sem("score_full")
        exp_done = sem("exp_done")
        sq_done = sem("sq_done")
        av_done = sem("av_done")
        o_copied = sem("o_copied")
        ot_ready = sem("ot_ready")
        rs_ready = sem("rs_ready")
        res_ready = sem("res_ready")
        x1_ready = sem("x1_ready")
        ln2_stats = sem("ln2_stats")
        ln2_rstd = sem("ln2_rstd")
        x2n_ready = sem("x2n_ready")
        x2T_ready = sem("x2T_ready")
        x1_stored = sem("x1_stored")
        x2n_stored = sem("x2n_stored")
        dve_step = sem("dve_step")
        pool_step = sem("pool_step")
        maxima_taken = sem("maxima_taken")
        exps_ready = sem("exps_ready")
        scores_ready = sem("scores_ready")
        copies_ready = sem("copies_ready")
        copies_turned = sem("copies_turned")
        highs_ready = sem("highs_ready")
        lows_ready = sem("lows_ready")
        tried_ready = sem("tried_ready")
        signs_summed = sem("signs_summed")
        tails_ready = sem("tails_ready")
        feasible = sem("feasible")
        counted = sem("counted")
        wide_ready = sem("wide_ready")
        thr_turned = sem("thr_turned")
        fresh_ready = sem("fresh_ready")
        same_ready = sem("same_ready")
        same_ranked = sem("same_ranked")
        taken_ready = sem("taken_ready")
        taken_ranked = sem("taken_ranked")
        slots_ready = sem("slots_ready")
        gates_split = sem("gates_split")
        w1_in = sem("w1_in")
        w2_in = sem("w2_in")
        b2_in = sem("b2_in")
        w1hi_ready = sem("w1hi_ready")
        w1lo_ready = sem("w1lo_ready")
        w2hi_ready = sem("w2hi_ready")
        w2lo_ready = sem("w2lo_ready")
        b1c_ready = sem("b1c_ready")
        hot_ready = sem("hot_ready")
        hot_hi_ready = sem("hot_hi_ready")
        values_ready = sem("values_ready")
        list_full = sem("list_full")
        list_ready = sem("list_ready")
        gathered = [sem("gathered0"), sem("gathered1")]
        x_turned = sem("x_turned")
        xhi_ready = sem("xhi_ready")
        xlo_ready = sem("xlo_ready")
        hidden_full = sem("hidden_full")
        gelu_done = sem("gelu_done")
        hid_ready = sem("hid_ready")
        y_full = sem("y_full")
        y_taken = sem("y_taken")
        y_ready = sem("y_ready")
        scattered = sem("scattered")
        carried = sem("carried")

        per_batch = {s.name: k for s, k in {
            xc_in[0]: 16, xc_in[1]: 16, xr_in: 32, ctx_in: 16, ln1_stats: 2, ln1_rstd: 2,
            xn_ready: 2, xnT_ready: 4, misc_full[0]: 15, misc_full[1]: 13,
            khi_ready: 2, klo_ready: 2, kbd_ready: 1, kst_ready: 1, logits_ready: 2, logT_ready: 2,
            **{s: 16 * 6 for s in ks_in}, v_staged: 1, v_ready: 1, qhi_ready: 4, qlo_ready: 4,
            q_stacked: 2 * 16 * 12, max_full: 48, max_free: 48, negmax_ready: 2,
            negmaxT_ready: 2, m_stacked[0]: 32, m_stacked[1]: 32, score_full: 48, exp_done: 48, sq_done: 32,
            av_done: 8, o_copied: 8, ot_ready: 8, rs_ready: 2, res_ready: 2, x1_ready: 2,
            ln2_stats: 2, ln2_rstd: 2, x2n_ready: 2, x2T_ready: 4, x1_stored: 32,
            x2n_stored: 32, dve_step: DVE_STEPS, pool_step: 4,
        }.items()} | {"quads": 2 * NQUAD}

        per_expert = {s.name: k for s, k in {
            w1_in: 16, w2_in: 16, b2_in: 16, w1hi_ready: PIECES, w1lo_ready: PIECES,
            w2hi_ready: PIECES, w2lo_ready: PIECES, b1c_ready: 1, hot_ready: HOTS,
            hot_hi_ready: 1, values_ready: 1, list_full: 1, list_ready: 1, gathered[0]: 8 * ST, gathered[1]: 8 * ST, x_turned: 4,
            xhi_ready: 4, xlo_ready: 4, hidden_full: 2 * MT, gelu_done: 2 * MT,
            hid_ready: 2 * MT, y_full: ST, y_taken: ST, y_ready: ST, scattered: 16 * ST,
            carried: 1 + ST, dve_step: EXPERT_STEPS,
        }.items()}

        def every_expert(tally, expert):
            tally.per_batch = per_expert
            expert(0, True)
            tally.loop(1, NE - 1, lambda e: expert(e, True))
            expert(NE - 1, False)

        def attention_over(engine):
            engine.wait_ge(logits_ready, NCH + PRIMED["logits_ready"])
            engine.wait_ge(x1_stored, 16 * NCH)
            engine.wait_ge(x2n_stored, 16 * NCH + PRIMED["x2n_stored"])

        def every_chunk(tally, chunk, straight=False):
            chunk(0, 0, 0, dict(prepare=True, finish=False, route=False, load=True))
            chunk(0, 1, 1, dict(prepare=True, finish=True, route=False, load=True))

            def batch(b):
                for c in range(2):
                    chunk(b, 2 * b + c, c, dict(prepare=True, finish=True, route=True, load=True))
            if straight:
                for b in range(1, B - 1):
                    batch(b)
            else:
                tally.loop(1, B - 1, batch)
            chunk(B - 1, NCH - 2, 0, dict(prepare=True, finish=True, route=True, load=False))
            chunk(B - 1, NCH - 1, 1, dict(prepare=False, finish=True, route=True, load=False))

        TILES = [(i, part) for i in range(2) for part in range(3)]

        block = ctx.enter_context(nc.Block())

        @block.sync
        def _(sp):
            tally = Tally(sp, per_batch)

            def load_x(g, parity):
                sp.dma_start(xc[:, parity], x_c[g]).then_inc(xc_in[parity], 16)

            def stack_queries(parity):
                tally.next(qhi_ready, KD)
                tally.next(qlo_ready, KD)
                for r in range(4):
                    for at, src in ((0, qhi), (32, qlo), (64, qhi)):
                        sp.dma_start(qs[parity][at:at + 32, r::4, :].bitcast(f32),
                                     src[32 * r:32 * r + 32, :, :].bitcast(f32)).then_inc(q_stacked, 16)

            def stack_maxima(parity):
                tally.next(negmaxT_ready)
                for half, (a, b) in enumerate(((0, 2), (2, NPAIR))):
                    sp.dma_start(qs[parity][96:128, a:b, :].bitcast(f32),
                                 negmaxT[:, :].bitcast(f32).rearrange("p (a c) -> p a c", a=1)
                                 .broadcast_to([32, b - a, CT])).then_inc(m_stacked[half], 16)

            def stack_keys(quad):
                for i in (2 * quad, 2 * quad + 1):
                    et, r = i // 4, i % 4
                    for at, src in ((0, kst[0]), (32, kst[0]), (64, kst[1])):
                        sp.dma_start(ks[at:at + 32, i, :].bitcast(f32),
                                     src[32 * r:32 * r + 32, et, :].bitcast(f32))\
                          .then_inc(ks_in[quad], 16)

            def load_context(b):
                sp.dma_start(ctxT[:, :, :], ctx_d[b].rearrange("(k p) n -> p k n", p=P))\
                  .then_inc(ctx_in, 16)

            load_x(0, 0)
            load_context(0)
            sp.dma_start(wk[:, :, :], wk_d.rearrange("(k p) e -> p k e", p=P)).then_inc(first_in, 16)
            sp.dma_start(cf[:, 0:C_VR], cf_d[:, 0:C_VR]).then_inc(first_in, 16)
            for w, src in ((bk, bk_d), (bq, bq_d)):
                sp.dma_start(w[:, :], src).then_inc(first_in, 16)
            for w, src in ((wq, wq_d), (wv, wv_d)):
                sp.dma_start(w[:, :, :], src.rearrange("(k p) e -> p k e", p=P))\
                  .then_inc(first_in, 16)
            sp.dma_start(cf[:, C_VR:C_ALL], cf_d[:, C_VR:C_ALL]).then_inc(late_in, 16)
            sp.dma_start(bv[:, :], bv_d.rearrange("(a n) -> a n", a=1).broadcast_to([P, D]))\
              .then_inc(late_in, 16)
            sp.dma_start(osb[:, 0, 0, 0:B_ALL], cb_d).then_inc(late_in, 16)
            sp.dma_start(wr[:, :, :], wr_d.rearrange("(k p) e -> p k e", p=P)).then_inc(late_in, 16)
            sp.dma_start(b1[:, :, :], b1_d).then_inc(late_in, 16)
            sp.dma_start(sq[96:128, 0:6, :].rearrange("p a c -> p (a c)"), ck_d)\
              .then_inc(ks_const_in, 16)
            load_x(1, 1)
            tally.next(kst_ready)
            for quad in (0, 1):
                stack_keys(quad)
            stack_queries(0)
            stack_maxima(0)
            for quad in (2, 3):
                stack_keys(quad)

            def chunk(b, g, parity, has):
                before = tally.n.get("score_full", 0)
                tally.add(xn_ready)
                if has["load"]:
                    tally.wait(xn_ready, tally.n["xn_ready"])
                    load_x(g + 2, parity)
                if has["finish"]:
                    if has["route"]:
                        tally.next(x1_ready)
                    sp.dma_start(xr[:, :, :], x_c[g - 1]).then_inc(xr_in, 16)
                if has["route"]:
                    sp.dma_start(out_c[g - 2], x1[:, :, :]).then_inc(x1_stored, 16)
                if parity == 0:
                    tally.next(v_staged)
                    if has["load"]:
                        load_context(b + 1)
                if has["prepare"]:
                    tally.wait(score_full, before)
                    stack_queries(1 - parity)
                tally.add(score_full, 24)
                if has["route"]:
                    tally.next(x2n_ready)
                    sp.dma_start(x2n_c[g - 2], x2n[:, :, :]).then_inc(x2n_stored, 16)
                if has["prepare"]:
                    if parity == 1:
                        tally.next(kst_ready)
                        for quad in (0, 1):
                            tally.wait(score_full, before + 6 * (quad + 1))
                            stack_keys(quad)
                    stack_maxima(1 - parity)
                    if parity == 1:
                        for quad in (2, 3):
                            tally.wait(score_full, before + 6 * (quad + 1))
                            stack_keys(quad)

            every_chunk(tally, chunk, straight=True)
            for g in (NCH - 2, NCH - 1):
                tally.next(x1_ready)
                if g == NCH - 2:
                    sp.dma_start(xr[:, :, :], x_c[NCH - 1]).then_inc(xr_in, 16)
                sp.dma_start(out_c[g], x1[:, :, :]).then_inc(x1_stored, 16)
                tally.next(x2n_ready)
                sp.dma_start(x2n_c[g], x2n[:, :, :]).then_inc(x2n_stored, 16)

            def load_w1(e):
                sp.dma_start(w1raw[:, :].rearrange("p (k n) -> p k n", k=KD),
                             w1_d[e].rearrange("(k p) n -> p k n", p=P)).then_inc(w1_in, 16)

            def load_w2(e):
                sp.dma_start(w2raw[:, :].rearrange("p (m n) -> p m n", m=MT),
                             w2_d[e].rearrange("(m p) n -> p m n", p=P)).then_inc(w2_in, 16)

            def load_b2(e):
                sp.dma_start(b2c[:, :], b2_d[e:e + 1, :].broadcast_to([P, D])).then_inc(b2_in, 16)

            attention_over(sp)
            load_w1(0)
            load_w2(0)
            load_b2(0)
            for e in range(1, NE):
                tally.next(w1hi_ready, PIECES)
                tally.next(w1lo_ready, PIECES)
                load_w1(e)
                tally.next(w2hi_ready, PIECES)
                tally.next(w2lo_ready, PIECES)
                load_w2(e)
                tally.next(y_taken, ST)
                load_b2(e)
            sp.wait_ge(scattered, NE * ST * 16)

        @block.scalar
        def _(act):
            tally = Tally(act, per_batch)

            def take(k):
                tally.next(misc_full[k])
                return MISC[k]

            def project_keys():
                filled = take(0)
                tally.wait(kst_ready, tally.add(kst_ready) - 1)
                for et in range(KD):
                    act.activation(khi[:, et, :], filled[:, et * 256:et * 256 + L2], ACT.Identity,
                                   bias=bk[:, et:et + 1]).then_inc(khi_ready, 1)
                    tally.add(khi_ready)

            def project_values():
                filled = take(1)
                tally.wait(v_ready, tally.add(v_staged) - 1)
                act.activation(vst[:, :, :], filled[:, :].rearrange("p (a e) -> p a e", a=2),
                               ACT.Copy).then_inc(v_staged, 1)

            def norm_turned():
                for d in range(KD):
                    act.activation(xnT[:, d, :], take(d)[:, :], ACT.Copy).then_inc(xnT_ready, 1)

            def queries():
                tally.wait(q_stacked, tally.n.get("q_stacked", 0))
                for et in range(KD):
                    act.activation(qhi[:, et, :], take(et)[:, :], ACT.Identity,
                                   bias=bq[:, et:et + 1]).then_inc(qhi_ready, 1)
                tally.add(q_stacked, 16 * 12)

            def maxima():
                filled = take(1)
                for s in m_stacked:
                    tally.wait(s, tally.n.get(s.name, 0))
                act.activation(negmaxT[:, :], filled[0:32, :], ACT.Copy).then_inc(negmaxT_ready, 1)
                for s in m_stacked:
                    tally.add(s, 16)

            def exponential(quad, n):
                i, part = TILES[n]
                if n == 0:
                    tally.wait(av_done, tally.add("quads") - 2)
                tally.next(score_full)
                scale = cf[:, C_ESC:C_ESC + 1] if part == 2 else SCALE
                act.activation(ex[:, (quad % 2) * 6 + n, :], SCB[n % 2][:, :], ACT.Exp, scale=scale)\
                   .then_inc(exp_done, 1)

            def outputs(quad, parity):
                tally.next(av_done)
                act.activation(osb[:, parity, quad, :], OB[:, :], ACT.Copy).then_inc(o_copied, 1)

            def outputs_turned(t):
                filled = take(t % 2)
                if t == 0:
                    tally.wait(res_ready, tally.add(res_ready) - 1)
                act.activation(ot[:, t * H:(t + 1) * H, :],
                               filled[:, :].rearrange("p (h r) -> p h r", r=32)[:, :, 0:DH + 1],
                               ACT.Copy).then_inc(ot_ready, 1)

            def route_turned():
                for d in range(KD):
                    act.activation(x2T[:, d, :], take(d)[:, :], ACT.Copy).then_inc(x2T_ready, 1)

            def router_logits():
                act.activation(logT[:, :], take(0)[:, 0:P], ACT.Copy).then_inc(logT_ready, 1)

            def logits_turned(g):
                act.activation(logits[:, bass.ds(g * TPC, TPC), :],
                               take(0)[:, P:2 * P].rearrange("p (t e) -> p t e", e=32)[:, :, 0:NE],
                               ACT.Copy).then_inc(logits_ready, 1)

            act.wait_ge(first_in, 16 * FIRST_LOADS)
            project_keys()
            project_values()
            norm_turned()
            queries()
            act.wait_ge(ks_const_in, 16)
            act.activation(ks[96:128, :, :].rearrange("p a c -> p (a c)"),
                           sq[96:128, 0:6, :].rearrange("p a c -> p (a c)"), ACT.Copy)\
               .then_inc(ks_const, 1)
            act.wait_ge(late_in, 16 * LATE_LOADS)
            act.activation(cb[:, :], osb[:, 0, 0, 0:B_ALL], ACT.Copy)
            maxima()

            def chunk(b, g, parity, has):
                for slot in range(3 * NQUAD):
                    quad, r = slot // 3, slot % 3
                    if r == 0 and (quad >= 2 or has["finish"]):
                        outputs((quad + 2) % NQUAD, parity if quad >= 2 else 1 - parity)
                    if has["prepare"] and slot == 9:
                        maxima()
                    for n in (2 * r, 2 * r + 1):
                        exponential(quad, n)
                    if has["prepare"]:
                        if slot == 0:
                            norm_turned()
                        if slot == 1:
                            queries()
                    if has["route"] and slot == 3:
                        route_turned()
                    if has["finish"] and 4 <= slot < 4 + TPC:
                        outputs_turned(slot - 4)
                    if has["route"] and slot == 8:
                        router_logits()
                    if has["route"] and slot == 9:
                        logits_turned(g - 2)
                    if parity == 0 and has["load"]:
                        if slot == 10:
                            project_keys()
                        if slot == 11:
                            project_values()

            every_chunk(tally, chunk)
            outputs(NQUAD - 2, 1)
            outputs(NQUAD - 1, 1)
            for t in range(TPC):
                outputs_turned(t)
            for g in (NCH - 2, NCH - 1):
                route_turned()
                router_logits()
                logits_turned(g)

            def split_w1(first=0, end=PIECES):
                if first == 0:
                    tally.next(w1_in, 16)
                n = KD * DI // PIECES
                for i in range(first, end):
                    act.activation(w1s[0][:, i * n:(i + 1) * n], w1raw[:, i * n:(i + 1) * n],
                                   ACT.Copy).then_inc(w1hi_ready, 1)

            attention_over(act)
            act.wait_ge(maxima_taken, 1)
            act.activation(exps[:, :, :], scores[:, :, :], ACT.Exp).then_inc(exps_ready, 1)
            act.wait_ge(scores_ready, 1)
            for k in range(1, NCH, 2):
                act.activation(copies[:, k * TPC:(k + 1) * TPC, :]
                               .rearrange("p t (e j) -> p t e j", e=NE),
                               scores[:, :, k * TPC:(k + 1) * TPC].rearrange("p e (t a) -> p t e a", a=1)
                               .broadcast_to([P, TPC, NE, P // NE]), ACT.Copy).then_inc(copies_ready, 1)
            for k in range(1, NCH, 2):
                act.wait_ge(copies_turned, k + 1)
                act.activation(highs[:, k * CT:(k + 1) * CT],
                               bank[k][:, :].bitcast(u16).rearrange("p (n a) -> p n a", a=2)[:, :, 1],
                               ACT.Copy).then_inc(highs_ready, 1)

            def take_lows(k):
                act.activation(lows[:, k * CT:(k + 1) * CT],
                               bank[k][:, :].bitcast(u16).rearrange("p (n a) -> p n a", a=2)[:, :, 0],
                               ACT.Copy).then_inc(lows_ready, 1)

            take_lows(1)
            act.wait_ge(highs_ready, NCH)
            for r in range(ROUNDS):
                act.wait_ge(tried_ready, r + 1)
                if r == HALF:
                    act.wait_ge(tails_ready, 1)
                act.activation(signs[:, :], (highs if r < HALF else tails)[:, SCAN:N], ACT.Sign,
                               bias=tried[:, 1:2], accum_out=count[:, 1:2]).then_inc(signs_summed, 1)
                if r < HALF - 1:
                    take_lows(2 * r + 3)
                if r >= HALF:
                    split_w1((r - HALF) * 2, (r - HALF) * 2 + 2)

            def split_w2(i):
                if i == 0:
                    tally.next(w2_in, 16)
                n = MT * D // PIECES
                act.activation(w2s[0][:, i * n:(i + 1) * n], w2raw[:, i * n:(i + 1) * n],
                               ACT.Copy).then_inc(w2hi_ready, 1)

            def split_x(g):
                h, d = g // KD, g % KD
                tally.next(x_turned)
                act.activation(xt[0][:, d, h * CT:(h + 1) * CT], TURNB[g % 2][:, :], ACT.Copy)\
                   .then_inc(xhi_ready, 1)

            def expert(e, has_next):
                for k in range(2 * MT):
                    tally.next(hidden_full)
                    if k == 0:
                        tally.next(b1c_ready)
                    tally.wait(hid_ready, tally.add(hid_ready) - 4)
                    act.activation(hact[:, k % 4, :], HIDB[k % 4][:, :], ACT.Gelu,
                                   bias=b1c[:, k % MT:k % MT + 1]).then_inc(gelu_done, 1)
                    if 3 <= k < 3 + PIECES:
                        split_w2(k - 3)
                if has_next:
                    split_w1()
                    for g in range(4):
                        split_x(g)

            for g in range(4):
                split_x(g)
            every_expert(tally, expert)

        @block.tensor
        def _(pe):
            tally = Tally(pe, per_batch)

            def so_far(*events):
                for s in events:
                    tally.wait(s, tally.n.get(s.name, 0))

            def project_keys():
                tally.next(ctx_in, 16)
                so_far(ot_ready, klo_ready, logits_ready)
                for et in range(KD):
                    for d in range(KD):
                        last = pe.matmul(MISC[0][:, et * 256:et * 256 + L2],
                                         wk[:, d, et * P:(et + 1) * P], ctxT[:, d, 0:L2],
                                         start=(d == 0), stop=(d == KD - 1))
                last.then_inc(misc_full[0], 1)
                tally.add(klo_ready, KD)
                tally.add(kbd_ready)

            def project_values():
                so_far(v_staged, negmaxT_ready, qlo_ready)
                for part, (a, b) in enumerate(((0, P), (L2, L2 + P))):
                    for d in range(KD):
                        last = pe.matmul(MISC[1][:, part * D:(part + 1) * D], ctxT[:, d, a:b],
                                         wv[:, d, :], start=(d == 0), stop=(d == KD - 1))
                last.then_inc(misc_full[1], 1)
                tally.add(v_staged)

            def turn(src, ready, k_ready, free):
                tally.next(ready)
                so_far(*free)
                for d in range(KD):
                    for t in range(TPC):
                        last = pe.transpose(MISC[d][:, t * P:(t + 1) * P],
                                            src[:, t, d * P:(d + 1) * P], ident)
                    last.then_inc(misc_full[d], 1)
                tally.add(k_ready, KD)

            def norm_turned():
                turn(xn, xn_ready, xnT_ready, (klo_ready, v_staged, ot_ready, logits_ready,
                                             negmaxT_ready))

            def queries():
                so_far(xnT_ready)
                for et in range(KD):
                    for d in range(KD):
                        last = pe.matmul(MISC[et][:, :], wq[:, d, et * P:(et + 1) * P],
                                         xnT[:, d, :], start=(d == 0), stop=(d == KD - 1))
                    last.then_inc(misc_full[et], 1)
                tally.add(qlo_ready, KD)

            GROUPS = [(t, et, j, n) for t in range(TPC) for et in range(KD) for j, n in MAX_GROUPS]

            def scores_for_maxima(first, end, banks=MAXB):
                for k in range(first, end):
                    t, et, j, n = GROUPS[k]
                    if k == 0:
                        tally.next(qhi_ready, KD)
                        tally.wait(kbd_ready, tally.n["kbd_ready"])
                    filled = tally.add(max_full)
                    tally.wait(max_free, filled - len(banks))
                    pe.matmul(banks[k % len(banks)][:, 0:n * L2], qhi[:, et, t * P:(t + 1) * P],
                              kbd[:, et, j:j + n, :].rearrange("p j n -> p (j n)"),
                              start=True, stop=True).then_inc(max_full, 1)

            def maxima():
                tally.next(negmax_ready)
                so_far(x2T_ready, qlo_ready, ot_ready, v_staged)
                for t in range(TPC):
                    last = pe.transpose(MISC[1][0:32, t * P:(t + 1) * P],
                                        negmax[:, t, :, :].rearrange("p a h -> p (a h)").bitcast(f32),
                                        ident)
                last.then_inc(misc_full[1], 1)
                tally.add(negmaxT_ready)

            def scores(quad, n, parity):
                i, part = TILES[n]
                pair = 2 * quad + i
                filled = tally.add(score_full)
                tally.wait(exp_done, filled - 2)
                pe.matmul(SCB[n % 2][:, :], ks[:, pair, part * P:(part + 1) * P],
                          qs[parity][:, pair, :], start=True, stop=True).then_inc(score_full, 1)

            def weighted(quad, r):
                base = tally.n.get("exp_done", 0)
                if r == 0:
                    tally.wait(o_copied, tally.n.get("o_copied", 0))
                for j in range(4):
                    h = 4 * quad + j
                    to = OB[32 * j:32 * j + 32, :]
                    if r == 0:
                        n = TILES.index((j // 2, j % 2))
                        tally.wait(exp_done, base + n + 1)
                        pe.matmul(to, vmain[:, h, :], ex[:, (quad % 2) * 6 + n, :], start=True,
                                  stop=False)
                    elif r == 1:
                        tally.next(sq_done)
                        pe.matmul(to, cf[:, C_SUM:C_SUM + 32], sq[:, (quad % 2) * 4 + j, :],
                                  start=False, stop=False)
                    else:
                        n = TILES.index((j // 2, 2))
                        tally.wait(exp_done, base + n + 1)
                        last = pe.matmul(to, vrem[:, h, :], ex[:, (quad % 2) * 6 + n, :],
                                         start=False, stop=True)
                if r == 2:
                    last.then_inc(av_done, 1)
                    tally.add(exp_done, 6)
                    tally.add(o_copied)

            def outputs_turned(t, parity):
                if t == 0:
                    so_far(o_copied, x2T_ready, qlo_ready)
                elif t == 1:
                    so_far(negmaxT_ready, x2T_ready)
                else:
                    tally.wait(ot_ready, tally.n["ot_ready"] - 1)
                for quad in range(NQUAD):
                    last = pe.transpose(MISC[t % 2][:, quad * P:(quad + 1) * P],
                                        osb[:, parity, quad, t * P:(t + 1) * P], ident)
                last.then_inc(misc_full[t % 2], 1)
                tally.add(ot_ready)

            def route_turned():
                turn(x2n, x2n_ready, x2T_ready, (qlo_ready, negmaxT_ready, logits_ready, ot_ready))

            def router_logits():
                so_far(x2T_ready, ot_ready)
                for d in range(KD):
                    for t in range(TPC):
                        last = pe.matmul(MISC[0][32 * t:32 * t + 32, 0:P], wr[:, d, :],
                                         x2T[:, d, t * P:(t + 1) * P], start=(d == 0),
                                         stop=(d == KD - 1))
                last.then_inc(misc_full[0], 1)

            def logits_turned():
                tally.next(logT_ready)
                pe.transpose(MISC[0][:, P:2 * P], logT[:, :], ident).then_inc(misc_full[0], 1)
                tally.add(logits_ready)

            pe.wait_ge(first_in, 16 * FIRST_LOADS)
            project_keys()
            project_values()
            norm_turned()
            queries()
            scores_for_maxima(0, len(GROUPS), MAXB_FIRST)
            maxima()
            pe.wait_ge(ks_const, 1)

            def chunk(b, g, parity, has):
                tally.next(q_stacked, 16 * 12)
                tally.next(m_stacked[0], 16)
                if parity == 0:
                    tally.add(v_ready)
                for slot in range(3 * NQUAD):
                    quad, r = slot // 3, slot % 3
                    if slot == 3:
                        tally.next(m_stacked[1], 16)
                    if r == 0 and parity == 0:
                        tally.next(ks_in[quad], 16 * 6)
                    k = 4 * (slot - 2) if has["prepare"] and 2 <= slot < 8 else None
                    scores(quad, 2 * r, parity)
                    if k is not None:
                        scores_for_maxima(k, k + 1)
                    scores(quad, 2 * r + 1, parity)
                    if has["prepare"]:
                        if slot == 0:
                            norm_turned()
                        if slot == 1:
                            queries()
                    if has["route"] and slot == 3:
                        route_turned()
                    if has["finish"] and 4 <= slot < 4 + TPC:
                        outputs_turned(slot - 4, 1 - parity)
                    if has["route"] and slot == 8:
                        router_logits()
                    if has["route"] and slot == 9:
                        logits_turned()
                    if parity == 0 and has["load"]:
                        if slot == 10:
                            project_keys()
                        if slot == 11:
                            project_values()
                    if k is not None:
                        scores_for_maxima(k + 1, k + 3)
                    if slot == 3 and parity == 0:
                        tally.wait(v_ready, tally.n["v_ready"])
                    if quad > 0 or has["finish"]:
                        weighted((quad - 1) % NQUAD, r)
                    if k is not None:
                        scores_for_maxima(k + 3, k + 4)
                    if has["prepare"] and slot == 8:
                        maxima()

            every_chunk(tally, chunk)
            for r in range(3):
                weighted(NQUAD - 1, r)
            for t in range(TPC):
                outputs_turned(t, 1)
            for g in (NCH - 2, NCH - 1):
                route_turned()
                router_logits()
                logits_turned()

            attention_over(pe)
            for k in range(NCH):
                pe.wait_ge(copies_ready, NCH)
                for t in range(TPC):
                    last = pe.transpose(bank[k][:, t * P:(t + 1) * P], copies[:, k * TPC + t, :],
                                        ident)
                last.then_inc(copies_turned, 1)
            pe.wait_ge(highs_ready, NCH)
            pe.wait_ge(lows_ready, 2)
            for r in range(ROUNDS):
                pe.wait_ge(feasible, r + 1)
                pe.matmul(bank[r % 2][:, 0:1], cf[:, C_BLOCK:C_BLOCK + P], count[:, 3:4], start=True,
                          stop=True).then_inc(counted, 1)
            pe.wait_ge(lows_ready, NCH)
            pe.wait_ge(wide_ready, 1)
            pe.transpose(bank[2][:, 0:P], wide[:, :], ident).then_inc(thr_turned, 1)

            def ranks(to, mask):
                pe.matmul(to[:, 0:NE * NT], cb[:, B_TRI:B_TRI + P],
                          mask[:, :, :].rearrange("p e t -> p (e t)"), start=True, stop=False)
                return pe.matmul(to[:, 0:NE * NT], cb[:, B_ONES:B_ONES + P],
                                 before[:, :, :].rearrange("p e t -> p (e t)"), start=False, stop=True)

            pe.wait_ge(same_ready, 1)
            pe.matmul(bank[3][:, 0:NE], cb[:, B_ONES:B_ONES + P], cum_over[:, :, NT - 1],
                      start=True, stop=True)
            ranks(bank[4], same).then_inc(same_ranked, 1)
            pe.wait_ge(taken_ready, 1)
            ranks(bank[5], taken).then_inc(taken_ranked, 1)

            SPLITS = ((0, 0), (0, 1), (1, 0))

            def list_tokens(t):
                if t == 0:
                    tally.next(values_ready)
                if t % (NT // HOTS) == 0:
                    tally.next(hot_ready)
                last = pe.matmul(LISTB[:, 0:ST * 5], hot_lo[:, t, :],
                                 values[:, t, :, :].rearrange("p k v -> p (k v)"),
                                 start=(t == 0), stop=(t == NT - 1))
                if t == NT - 1:
                    last.then_inc(list_full, 1)

            def turn_x(g):
                h, d = g // KD, g % KD
                if d == 0:
                    tally.next(gathered[h], 8 * ST)
                tally.wait(xlo_ready, tally.add(xlo_ready) - 2)
                for t in range(TPC):
                    last = pe.transpose(TURNB[g % 2][:, t * P:(t + 1) * P],
                                        xg[:, h * TPC + t, d * P:(d + 1) * P], ident)
                last.then_inc(x_turned, 1)

            def expert(e, has_next):
                for k in range(2 * MT):
                    h, m = k // MT, k % MT
                    if k == 0:
                        tally.next(w1hi_ready, PIECES)
                        tally.next(w1lo_ready, PIECES)
                        tally.wait(xlo_ready, tally.n["xlo_ready"] - 2)
                    if k == 3:
                        tally.wait(xlo_ready, tally.n["xlo_ready"])
                    tally.wait(gelu_done, tally.add(gelu_done) - 4)
                    for i, (a, b) in enumerate(SPLITS):
                        for d in range(KD):
                            at = d * DI + m * P
                            last = pe.matmul(HIDB[k % 4][:, :], w1s[a][:, at:at + P],
                                             xt[b][:, d, h * CT:(h + 1) * CT],
                                             start=(i == 0 and d == 0), stop=(i == 2 and d == KD - 1))
                    last.then_inc(hidden_full, 1)
                    if has_next and 0 <= k - LISTS_AT < HOTS:
                        for t in range(NT // HOTS):
                            list_tokens((k - LISTS_AT) * (NT // HOTS) + t)
                for n in range(ST):
                    if n == 0:
                        tally.next(w2hi_ready, PIECES)
                        tally.next(w2lo_ready, PIECES)
                    if n % TPC == 0:
                        tally.next(hid_ready, MT)
                    tally.wait(y_taken, tally.add(y_taken) - 2)
                    for m in range(MT):
                        for i, (a, b) in enumerate(SPLITS):
                            last = pe.matmul(YB[n % 2][:, 0:D], hid[a][:, m, n * P:(n + 1) * P],
                                             w2s[b][:, m * D:(m + 1) * D],
                                             start=(m == 0 and i == 0), stop=(m == MT - 1 and i == 2))
                    last.then_inc(y_full, 1)
                    if has_next and 3 <= n < 7:
                        turn_x(n - 3)

            for t in range(NT):
                list_tokens(t)
            for g in range(4):
                turn_x(g)
            every_expert(tally, expert)

        @block.vector
        def _(dve):
            tally = Tally(dve, per_batch)

            def step(ins):
                ins.then_inc(dve_step, 1)
                tally.add(dve_step)

            def settle():
                tally.wait(dve_step, tally.n["dve_step"])

            def so_far(*events):
                for s in events:
                    tally.wait(s, tally.n.get(s.name, 0))

            def statistics(k, src, done):
                for t in range(TPC):
                    step(dve.bn_stats(bn[:, k, t, :], src[:, t, :]))
                settle()
                dve.memset(idle[:, :], 0.0)
                for t in range(TPC):
                    last = dve.bn_aggr(mv[:, k, t, :], bn[:, k, t, :])
                last.then_inc(done, 1)
                tally.add(done)

            def normalise(k, to, src, rstd_sem, done):
                tally.next(rstd_sem)
                for t in range(TPC):
                    last = dve.tensor_scalar(to[:, t, :], src[:, t, :], mv[:, k, t, 0:1],
                                             rstd[:, k, t:t + 1], ALU.subtract, ALU.mult)
                last.then_inc(done, 1)
                tally.add(done)

            def first_statistics(parity):
                tally.next(xc_in[parity], 16)
                statistics(0, xc[:, parity], ln1_stats)

            def first_norm(parity):
                so_far(xnT_ready)
                normalise(0, xn, xc[:, parity], ln1_rstd, xn_ready)
                tally.add(xnT_ready, KD)

            def keys():
                tally.next(khi_ready, KD)
                for et in range(KD):
                    dve.scalar_tensor_tensor(klo[:, et, :], MISC[0][:, et * 256:et * 256 + L2],
                                             bk[:, et:et + 1], khi[:, et, :].bitcast(f32),
                                             ALU.add, ALU.subtract).then_inc(klo_ready, 1)
                    tally.add(klo_ready)

            def stage_keys():
                tally.wait(klo_ready, tally.n["klo_ready"])
                for j in range(HPT):
                    last = dve.tensor_scalar(kbd[:, :, j, :], khi[:, :, :].bitcast(f32),
                                             cf[:, C_HEAD + j:C_HEAD + j + 1], None, ALU.mult)
                last.then_inc(kbd_ready, 1)
                so_far(*ks_in)
                for part, src in enumerate((khi, klo)):
                    for s in range(2):
                        own = cf[:, C_HALF + s:C_HALF + s + 1]
                        dve.tensor_scalar(kst[part][:, :, s * P:(s + 1) * P],
                                          src[:, :, 0:P].bitcast(f32), own, None, ALU.mult)
                        for at in (0, 32):
                            a = 2 * P + 64 * s + at
                            last = dve.tensor_scalar(kst[part][:, :, a:a + REM],
                                                     src[:, :, P:L2].bitcast(f32), own, None,
                                                     ALU.mult)
                last.then_inc(kst_ready, 1)
                for s in ks_in:
                    tally.add(s, 16 * 6)

            def values():
                tally.next(v_staged)
                so_far(av_done)
                bvh = bv[:, :].rearrange("p (h d) -> p h d", d=DH)
                vs = [vst[:, i, :].rearrange("p (h d) -> p h d", d=DH) for i in range(2)]
                dve.tensor_tensor(vmain[:, :, 0:DH], vs[0], bvh, ALU.add)
                for s in range(2):
                    rows = slice(64 * s, 64 * s + REM)
                    last = dve.tensor_tensor(vrem[rows, s::2, 0:DH], vs[1][rows, s::2, :],
                                             bvh[rows, s::2, :], ALU.add)
                last.then_inc(v_ready, 1)

            def queries():
                so_far(q_stacked)
                for et in range(KD):
                    tally.next(qhi_ready)
                    dve.scalar_tensor_tensor(qlo[:, et, :], MISC[et][:, :], bq[:, et:et + 1],
                                             qhi[:, et, :].bitcast(f32), ALU.add, ALU.subtract)\
                       .then_inc(qlo_ready, 1)
                tally.add(q_stacked, 16 * 12)

            def maxima(place_values=False, banks=MAXB):
                k = 0
                for t in range(TPC):
                    for et in range(KD):
                        for j, n in MAX_GROUPS:
                            tally.next(max_full)
                            dve.tensor_reduce(maxes[:, t, et * HPT + j:et * HPT + j + n],
                                              banks[k % len(banks)][:, 0:n * L2]
                                              .rearrange("p (j n) -> p j n", n=L2), AX, ALU.max)\
                               .then_inc(max_free, 1)
                            tally.add(max_free)
                            k += 1
                            if place_values and k == 4:
                                values()
                so_far(max_free, negmaxT_ready)
                step(dve.tensor_scalar(negmax[:, :, 0, :], maxes[:, :, :], -1.0, None, ALU.mult))
                settle()
                dve.scalar_tensor_tensor(negmax[:, :, 1, :], maxes[:, :, :], -1.0,
                                         negmax[:, :, 0, :].bitcast(f32), ALU.mult,
                                         ALU.subtract).then_inc(negmax_ready, 1)
                tally.add(negmaxT_ready)

            def rescale():
                tally.next(ot_ready, TPC)
                so_far(res_ready)
                ss = ot[:, :, DH]
                step(dve.tensor_scalar(ri[:, :], ss.bitcast(i32), 1, None, ALU.logical_shift_right))
                settle()
                step(dve.tensor_scalar(rs[:, :].bitcast(i32), ri[:, :], -1.0, float(RSQRT_SEED),
                                       ALU.mult, ALU.add))
                settle()
                for n in range(3):
                    step(dve.scalar_tensor_tensor(rt[:, :], rs[:, :], -0.5, rs[:, :], ALU.mult,
                                                  ALU.mult))
                    settle()
                    step(dve.tensor_tensor(rt[:, :], rt[:, :], ss, ALU.mult))
                    settle()
                    last = dve.scalar_tensor_tensor(rs[:, :], rt[:, :], 1.5, rs[:, :], ALU.add,
                                                    ALU.mult)
                    if n < 2:
                        step(last)
                        settle()
                last.then_inc(rs_ready, 1)
                tally.add(rs_ready)
                tally.add(res_ready)

            def residual():
                so_far(res_ready, x1_stored)
                tally.next(xr_in, 16)
                dve.tensor_tensor(x1[:, :, :].rearrange("p t d -> p (t d)"),
                                  res[:, :, :].rearrange("p h d -> p (h d)"),
                                  xr[:, :, :].rearrange("p t d -> p (t d)"), ALU.add)\
                   .then_inc(x1_ready, 1)
                tally.add(x1_ready)
                tally.add(x1_stored, 16)
                so_far(x1_ready)
                statistics(1, x1, ln2_stats)

            def second_norm():
                so_far(x2n_stored, x2T_ready)
                normalise(1, x2n, x1, ln2_rstd, x2n_ready)
                tally.add(x2n_stored, 16)
                tally.add(x2T_ready, KD)

            dve.memset(vmain[:, :, :].rearrange("p h r -> p (h r)"), 0.0)
            first_statistics(0)
            first_norm(0)
            dve.wait_ge(first_in, 16 * FIRST_LOADS)
            keys()
            dve.wait_ge(kst_clear, 1)
            stage_keys()
            queries()
            maxima(banks=MAXB_FIRST)
            dve.wait_ge(late_in, 16 * LATE_LOADS)
            dve.tensor_copy(vrem[:, :, :].rearrange("p h r -> p (h r)"), cf[:, C_VR:C_VR + H * 32])\
               .then_inc(vrem_const, 1)
            dve.wait_ge(vrem_const, 1)
            values()
            first_statistics(1)
            first_norm(1)

            def chunk(b, g, parity, has):
                if has["route"]:
                    second_norm()
                if has["prepare"]:
                    queries()
                if has["finish"]:
                    tally.add(av_done, NQUAD)
                if has["prepare"]:
                    maxima(place_values=(parity == 0 and has["finish"]))
                if has["load"]:
                    first_statistics(parity)
                if has["finish"]:
                    rescale()
                if has["load"]:
                    first_norm(parity)
                    if parity == 0:
                        keys()
                if has["finish"]:
                    residual()
                if has["load"] and parity == 0:
                    stage_keys()

            every_chunk(tally, chunk)
            second_norm()
            rescale()
            so_far(rs_ready, x1_ready)
            dve.tensor_tensor(res[:, :, :], ot[:, :, 0:DH],
                              rs[:, :].rearrange("p (h a) -> p h a", a=1)
                              .broadcast_to([P, TPC * H, DH]), ALU.mult).then_inc(res_ready, 1)
            residual()
            second_norm()

            attention_over(dve)
            settle()
            over_t = [P, NE, NT]
            turned = logits[:, :, :].rearrange("p t e -> p e t")
            step(dve.tensor_reduce(best[:, 0, :], logits[:, :, :], AX, ALU.max))
            settle()
            dve.tensor_tensor(scores[:, :, :], turned,
                              best[:, 0:1, :].broadcast_to(over_t), ALU.subtract)\
               .then_inc(maxima_taken, 1)
            dve.wait_ge(exps_ready, 1)
            step(dve.tensor_reduce(best[:, 1, :], exps[:, :, :].rearrange("p e t -> p t e"), AX,
                                   ALU.add))
            settle()
            step(dve.reciprocal(best[:, 2, :], best[:, 1, :]))
            settle()
            dve.tensor_tensor(scores[:, :, :], exps[:, :, :],
                              best[:, 2:3, :].broadcast_to(over_t), ALU.mult)\
               .then_inc(scores_ready, 1)
            dve.wait_ge(scores_ready, 1)
            for k in range(0, NCH, 2):
                dve.tensor_copy(copies[:, k * TPC:(k + 1) * TPC, :]
                                .rearrange("p t (e j) -> p t e j", e=NE),
                                scores[:, :, k * TPC:(k + 1) * TPC].rearrange("p e (t a) -> p t e a", a=1)
                                .broadcast_to([P, TPC, NE, P // NE])).then_inc(copies_ready, 1)
            dve.tensor_copy(tried[:, 0:1], cf[:, C_CAND:C_CAND + 1])
            dve.tensor_scalar(tried[:, 1:2], cf[:, C_CAND:C_CAND + 1], -1.0, 0.5, ALU.mult, ALU.add)\
               .then_inc(tried_ready, 1)
            dve.memset(found[:, :], 0.0)
            for k in range(0, NCH, 2):
                dve.wait_ge(copies_turned, k + 1)
                dve.tensor_copy(highs[:, k * CT:(k + 1) * CT],
                                bank[k][:, :].bitcast(u16).rearrange("p (n a) -> p n a", a=2)[:, :, 1])\
                   .then_inc(highs_ready, 1)

            def take_lows(k):
                dve.tensor_copy(lows[:, k * CT:(k + 1) * CT],
                                bank[k][:, :].bitcast(u16).rearrange("p (n a) -> p n a", a=2)[:, :, 0])\
                   .then_inc(lows_ready, 1)

            take_lows(0)
            dve.wait_ge(highs_ready, NCH)

            def low_w(i, raw, parts, hi_ready, lo_ready):
                n = raw.shape[1] // PIECES
                tally.next(hi_ready)
                cols = slice(i * n, (i + 1) * n)
                dve.tensor_tensor(parts[1][:, cols], raw[:, cols], parts[0][:, cols].bitcast(f32),
                                  ALU.subtract).then_inc(lo_ready, 1)

            for r in range(ROUNDS):
                half, grain = r // HALF, float(1 << SHIFTS[r])
                more = r % HALF < HALF - 1
                own = found[:, half:half + 1]
                if r == HALF:
                    high = found[:, 0:1]
                    dve.wait_ge(lows_ready, NCH)
                    dve.tensor_scalar(greater[:, :], highs[:, :], high, 65535.0, ALU.is_gt, ALU.mult)
                    step(dve.tensor_scalar(equal[:, :], highs[:, :], high, None, ALU.is_equal))
                    settle()
                    step(dve.tensor_tensor(tails[:, :], equal[:, :], lows[:, :], ALU.mult))
                    settle()
                    dve.tensor_tensor(tails[:, :], tails[:, :], greater[:, :], ALU.add)\
                       .then_inc(tails_ready, 1)
                    dve.wait_ge(tails_ready, 1)
                step(dve.tensor_scalar(above[:, :], (tails if half else highs)[:, 0:SCAN],
                                       tried[:, 0:1], 0.0, ALU.is_ge, ALU.add,
                                       accum_out=count[:, 0:1]))
                settle()
                step(dve.tensor_scalar(count[:, 2:3], count[:, 0:1], -2.0,
                                       float(2 * CAP - (N - SCAN)), ALU.mult, ALU.add))
                settle()
                dve.wait_ge(signs_summed, r + 1)
                dve.tensor_tensor(count[:, 3:4], count[:, 1:2], count[:, 2:3], ALU.is_ge)\
                   .then_inc(feasible, 1)
                step(dve.tensor_scalar(base[:, 0:1], own, -grain, None, ALU.add))
                settle()
                if more:
                    step(dve.tensor_tensor(base[:, 1:2], base[:, 0:1],
                                           cf[:, C_CAND + r + 1:C_CAND + r + 2], ALU.add))
                    settle()
                    step(dve.tensor_scalar(base[:, 2:3], base[:, 1:2], -1.0, 0.5, ALU.mult, ALU.add))
                    settle()
                if r < HALF - 1:
                    take_lows(2 * r + 2)
                if r >= HALF:
                    for i in (2 * (r - HALF), 2 * (r - HALF) + 1):
                        low_w(i, w1raw, w1s, w1hi_ready, w1lo_ready)
                dve.wait_ge(counted, r + 1)
                grain *= 0.25 if r == HALF - 1 else 1.0
                if more:
                    for i, way in ((1, -1.0), (0, 1.0)):
                        last = dve.scalar_tensor_tensor(tried[:, i:i + 1], bank[r % 2][:, 0:1],
                                                        way * grain, base[:, 1 + i:2 + i], ALU.mult,
                                                        ALU.add)
                    last.then_inc(tried_ready, 1)
                elif r < ROUNDS - 1:
                    dve.tensor_copy(tried[:, 0:1], cf[:, C_CAND + r + 1:C_CAND + r + 2])
                    dve.tensor_scalar(tried[:, 1:2], cf[:, C_CAND + r + 1:C_CAND + r + 2], -1.0, 0.5,
                                      ALU.mult, ALU.add).then_inc(tried_ready, 1)
                step(dve.scalar_tensor_tensor(own, bank[r % 2][:, 0:1], grain, base[:, 0:1], ALU.mult,
                                              ALU.add))
                settle()
            step(dve.tensor_copy(foundi[:, 0:2], found[:, :]))
            settle()
            step(dve.tensor_scalar(foundi[:, 2:3], foundi[:, 0:1], 16, None, ALU.logical_shift_left))
            settle()
            step(dve.tensor_tensor(foundi[:, 2:3], foundi[:, 2:3], foundi[:, 1:2], ALU.bitwise_or))
            settle()

            dve.tensor_copy(wide[:, :], foundi[:, 2:3].bitcast(f32).broadcast_to([P, P]))\
               .then_inc(wide_ready, 1)
            dve.wait_ge(thr_turned, 1)
            step(dve.tensor_copy(thr[:, :], bank[2][:, 0:P:P // NE]))
            settle()
            at_thr = thr[:, :].rearrange("p (e a) -> p e a", a=1).broadcast_to(over_t)
            flat = "p e t -> p (e t)"

            def running(to, mask):
                return dve.tensor_tensor_scan(to[:, :, :].rearrange(flat), fresh[:, :],
                                              mask[:, :, :].rearrange(flat), 0.0, ALU.mult, ALU.add)

            dve.tensor_tensor(over[:, :, :], scores[:, :, :], at_thr, ALU.is_gt)
            step(dve.tensor_tensor(same[:, :, :], scores[:, :, :], at_thr, ALU.is_equal))
            settle()
            dve.wait_ge(fresh_ready, 1)
            running(cum_over, over)
            step(running(cum, same))
            settle()
            dve.tensor_tensor(before[:, :, :], cum[:, :, :], same[:, :, :], ALU.subtract)\
               .then_inc(same_ready, 1)
            dve.wait_ge(same_ranked, 1)
            step(dve.tensor_scalar(need[:, :], bank[3][:, 0:NE], -1.0, float(CAP), ALU.mult, ALU.add))
            settle()
            step(dve.tensor_tensor(taken[:, :, :], bank[4][:, 0:NE * NT].rearrange("p (e t) -> p e t", e=NE),
                                   need[:, :].rearrange("p (e a) -> p e a", a=1).broadcast_to(over_t),
                                   ALU.is_lt))
            settle()
            step(dve.tensor_tensor(taken[:, :, :], taken[:, :, :], same[:, :, :], ALU.mult))
            settle()
            step(dve.tensor_tensor(taken[:, :, :], taken[:, :, :], over[:, :, :], ALU.add))
            settle()
            step(running(cum, taken))
            settle()
            dve.tensor_tensor(before[:, :, :], cum[:, :, :], taken[:, :, :], ALU.subtract)\
               .then_inc(taken_ready, 1)
            dve.wait_ge(taken_ranked, 1)
            step(dve.tensor_copy(slot[:, 0, :, :].rearrange(flat), bank[5][:, 0:NE * NT]))
            settle()
            dve.tensor_scalar(slot[:, 1, :, :], slot[:, 0, :, :], P - 1, None, ALU.bitwise_and)
            dve.tensor_scalar(slot[:, 2, :, :], slot[:, 0, :, :], 7, None, ALU.logical_shift_right)
            step(dve.tensor_scalar(exps[:, :, :], taken[:, :, :], -1000.0, 1000.0, ALU.mult, ALU.add))
            settle()
            dve.tensor_copy(slot_hi[:, :, :], slot[:, 2, :, :])
            step(dve.tensor_copy(slot_lo[:, :, :], slot[:, 1, :, :]))
            settle()
            dve.tensor_tensor(slot_lo[:, :, :], slot_lo[:, :, :], exps[:, :, :], ALU.add)\
               .then_inc(slots_ready, 1)
            dve.wait_ge(slots_ready, 1)

            def hot_slots(e, i):
                n = NT // HOTS
                dve.tensor_tensor(hot_lo[:, i * n:(i + 1) * n, :],
                                  cb[:, B_IOTA:B_IOTA + P].rearrange("p (a k) -> p a k", a=1)
                                  .broadcast_to([P, n, P]),
                                  slot_lo[:, e, i * n:(i + 1) * n].rearrange("p (t a) -> p t a", a=1)
                                  .broadcast_to([P, n, P]), ALU.is_equal).then_inc(hot_ready, 1)

            def high_slots(e):
                so_far(values_ready)
                dve.tensor_tensor(hot_hi[:, :, :],
                                  cb[:, B_IOTA8:B_IOTA8 + ST].rearrange("p (a k) -> p a k", a=1)
                                  .broadcast_to([P, NT, ST]),
                                  slot_hi[:, e, :].rearrange("p (t a) -> p t a", a=1)
                                  .broadcast_to([P, NT, ST]), ALU.is_equal).then_inc(hot_hi_ready, 1)
                tally.add(values_ready)

            def take_list():
                tally.next(list_full)
                step(dve.tensor_copy(packed[:, :, :].rearrange("p k v -> p (k v)"),
                                     LISTB[:, 0:ST * 5]))
                settle()
                so_far(*gathered)
                step(dve.tensor_tensor(gate_next[:, :], packed[:, :, 3], packed[:, :, 4], ALU.add))
                settle()
                dve.tensor_tensor(gate_next[:, :], gate_next[:, :], packed[:, :, 2], ALU.add)
                dve.scalar_tensor_tensor(tok_next[:, :], packed[:, :, 1], float(P), packed[:, :, 0],
                                         ALU.mult, ALU.add).then_inc(list_ready, 1)
                tally.add(list_ready)
                for s in gathered:
                    tally.add(s, 8 * ST)

            def keep_list():
                so_far(list_ready)
                so_far(scattered)
                dve.tensor_copy(tok_now[:, :], tok_next[:, :])
                step(dve.tensor_copy(gate_now[:, :], gate_next[:, :]))
                settle()
                tally.add(scattered, 16 * ST)

            def take_bias(e):
                dve.tensor_copy(b1c[:, :], b1[:, e, :]).then_inc(b1c_ready, 1)

            def low_x(g):
                h, d = g // KD, g % KD
                tally.next(xhi_ready)
                cols = slice(h * CT, (h + 1) * CT)
                dve.tensor_tensor(xt[1][:, d, cols], TURNB[g % 2][:, :],
                                  xt[0][:, d, cols].bitcast(f32), ALU.subtract).then_inc(xlo_ready, 1)

            def expert(e, has_next):
                for k in range(2 * MT):
                    h, m = k // MT, k % MT
                    cols = slice(h * CT, (h + 1) * CT)
                    tally.next(gelu_done)
                    step(dve.tensor_copy(hid[0][:, m, cols], hact[:, k % 4, :]))
                    if has_next and k == 0:
                        high_slots(e + 1)
                    if has_next and k < HOTS:
                        hot_slots(e + 1, k)
                    if 4 <= k < 4 + PIECES:
                        low_w(k - 4, w2raw, w2s, w2hi_ready, w2lo_ready)
                    settle()
                    dve.tensor_tensor(hid[1][:, m, cols], hact[:, k % 4, :],
                                      hid[0][:, m, cols].bitcast(f32), ALU.subtract)\
                       .then_inc(hid_ready, 1)
                    if k == 7:
                        keep_list()
                    if has_next and k == LISTS_AT + HOTS:
                        take_list()
                if has_next:
                    take_bias(e + 1)
                for n in range(ST):
                    if n == 0:
                        tally.next(b2_in, 16)
                    tally.next(y_full)
                    dve.tensor_tensor(y[:, n, :], YB[n % 2][:, 0:D], b2c[:, :], ALU.add)\
                       .then_inc(y_taken, 1)
                    if has_next and n < PIECES // 2:
                        for i in (2 * n, 2 * n + 1):
                            low_w(i, w1raw, w1s, w1hi_ready, w1lo_ready)
                    tally.next(y_taken)
                    dve.tensor_scalar(y[:, n, :], y[:, n, :], gate_now[:, n:n + 1], None, ALU.mult)\
                       .then_inc(y_ready, 1)
                    if has_next and 3 <= n < 7:
                        low_x(n - 3)

            high_slots(0)
            for i in range(HOTS):
                hot_slots(0, i)
            take_bias(0)
            take_list()
            for g in range(4):
                low_x(g)
            every_expert(tally, expert)

        @block.gpsimd
        def _(pool):
            tally = Tally(pool, per_batch)

            def so_far(*events):
                for s in events:
                    tally.wait(s, tally.n.get(s.name, 0))

            def deviations(k, stats, done):
                tally.next(stats)
                pool.tensor_tensor(veps[:, k, :], mv[:, k, :, 1], eps[:, :], ALU.add)\
                    .then_inc(pool_step, 1)
                tally.next(pool_step)
                pool.tensor_tensor(rstd[:, k, :], veps[:, k, :], minus_half[:, :], ALU.pow)\
                    .then_inc(done, 1)

            def squares(quad, between=None):
                tally.wait(av_done, tally.add("quads") - 2)
                base = tally.n.get("exp_done", 0)
                for i in range(2):
                    for part in range(2):
                        n = TILES.index((i, part))
                        tally.wait(exp_done, base + n + 1)
                        e = ex[:, (quad % 2) * 6 + n, :]
                        pool.tensor_tensor(sq[:, (quad % 2) * 4 + 2 * i + part, :], e, e, ALU.mult)\
                            .then_inc(sq_done, 1)
                        if between and (i, part) == (0, 1):
                            between()
                tally.add(exp_done, 6)

            def rescaled():
                tally.next(rs_ready)
                so_far(x1_ready)
                pool.tensor_tensor(res[:, :, :], ot[:, :, 0:DH],
                                   rs[:, :].rearrange("p (h a) -> p h a", a=1)
                                   .broadcast_to([P, TPC * H, DH]), ALU.mult).then_inc(res_ready, 1)
                tally.add(x1_ready)

            pool.memset(eps[:, :], EPS).then_inc(logits_ready, PRIMED["logits_ready"])
            pool.memset(minus_half[:, :], -0.5).then_inc(x2T_ready, PRIMED["x2T_ready"])
            pool.memset(kst[0][:, :, :].bitcast(f32), 0.0).then_inc(x2n_stored, PRIMED["x2n_stored"])
            pool.memset(kst[1][:, :, :].bitcast(f32), 0.0).then_inc(kst_clear, 1)
            pool.wait_ge(kst_clear, 1)
            deviations(0, ln1_stats, ln1_rstd)
            pool.wait_ge(ks_const, 1)
            deviations(0, ln1_stats, ln1_rstd)

            def chunk(b, g, parity, has):
                for quad in range(NQUAD - 1):
                    squares(quad)
                if has["load"]:
                    deviations(0, ln1_stats, ln1_rstd)
                squares(NQUAD - 1, between=rescaled if has["finish"] else None)
                if has["finish"]:
                    deviations(1, ln2_stats, ln2_rstd)

            every_chunk(tally, chunk)
            deviations(1, ln2_stats, ln2_rstd)

            attention_over(pool)
            pool.memset(fresh[:, :].rearrange("p (e t) -> p e t", e=NE)[:, :, 1:NT], 1.0)
            pool.memset(fresh[:, 0:NE * NT:NT], 0.0).then_inc(fresh_ready, 1)
            pool.memset(carrier[:, 0:1], 0.0)
            pool.wait_ge(scores_ready, 1)
            rest = scores
            for i in range(3):
                pool.tensor_copy(gate3[:, :, :, i], rest[:, :, :]).then_inc(gates_split, 1)
                pool.wait_ge(gates_split, 2 * i + 1)
                if i < 2:
                    pool.tensor_tensor(gate_rest[:, :, :], rest[:, :, :], gate3[:, :, :, i],
                                       ALU.subtract).then_inc(gates_split, 1)
                    pool.wait_ge(gates_split, 2 * i + 2)
                rest = gate_rest

            def list_values(e):
                so_far(list_full)
                tally.next(hot_hi_ready)
                for first, n, src in ((0, 2, cb[:, B_TOK:B_TOK + 2 * NT]
                                       .rearrange("p (t a v) -> p t a v", a=1, v=2)),
                                      (2, 3, gate3[:, e, :, :].rearrange("p t (a v) -> p t a v", a=1))):
                    last = pool.tensor_tensor(values[:, :, :, first:first + n],
                                              hot_hi[:, :, :].rearrange("p t (k a) -> p t k a", a=1)
                                              .broadcast_to([P, NT, ST, n]),
                                              src.broadcast_to([P, NT, ST, n]), ALU.mult)
                last.then_inc(values_ready, 1)
                tally.add(list_full)

            def carry():
                so_far(carried)
                pool.tensor_tensor(carrier[:, 1:2], carrier[:, 0:1], carrier[:, 0:1], ALU.mult)\
                    .then_inc(carried, 1)
                tally.add(carried)

            def gather():
                tally.next(list_ready)
                so_far(x_turned)
                carry()
                for n in range(ST):
                    pool.indirect_dma_start(xg[:, n, :], None, x2n_rows[:, :],
                                            bass.IndirectOffsetOnAxis(tok_next[:, n:n + 1], axis=0))\
                        .then_inc(gathered[n // TPC], 16)
                tally.add(x_turned, 4)

            def scatter():
                for n in range(ST):
                    tally.next(y_ready)
                    carry()
                    pool.indirect_dma_start(out_d[:, :],
                                            bass.IndirectOffsetOnAxis(tok_now[:, n:n + 1], axis=0),
                                            y[:, n, :], None, compute_op=ALU.add)\
                        .then_inc(scattered, 16)

            def expert(e, has_next):
                if has_next:
                    list_values(e + 1)
                    gather()
                scatter()

            pool.wait_ge(slots_ready, 1)
            list_values(0)
            gather()
            every_expert(tally, expert)


def kernel(x, ctx_1024, L0_xattn_Wq, L0_xattn_bq, L0_xattn_Wk, L0_xattn_bk, L0_xattn_Wv, L0_xattn_bv,
           L0_ffn_Wr, L0_ffn_W1, L0_ffn_b1, L0_ffn_W2, L0_ffn_b2):
    import numpy as _np
    import concourse.bacc as _bacc
    from concourse import mybir as _mybir
    from concourse.bass_utils import run_bass_kernel_spmd as _run

    def array(a):
        return _np.ascontiguousarray(_np.asarray(a))

    context = array(ctx_1024).transpose(0, 2, 1)
    columns = _np.zeros((B, D, L2 + P), context.dtype)
    columns[:, :, :L2] = context
    columns[:, :, L2:L2 + REM] = context[:, :, P:]
    columns[:, :, L2 + 64:L2 + 64 + REM] = context[:, :, P:]
    router = _np.zeros((D, 32), array(L0_ffn_Wr).dtype)
    router[:, :NE] = array(L0_ffn_Wr)
    cf, cb, ck = constants()
    arrays = {
        "x": array(x).reshape(N, D),
        "ctx": columns,
        "wq": array(array(L0_xattn_Wq).T), "wk": array(array(L0_xattn_Wk).T),
        "wv": array(array(L0_xattn_Wv).T),
        "bq": array(array(L0_xattn_bq).reshape(KD, P).T),
        "bk": array(array(L0_xattn_bk).reshape(KD, P).T),
        "bv": array(L0_xattn_bv),
        "wr": router,
        "w1": array(L0_ffn_W1),
        "b1": array(array(L0_ffn_b1).reshape(NE, MT, P).transpose(2, 0, 1)),
        "w2": array(L0_ffn_W2), "b2": array(L0_ffn_b2),
        "cf": cf, "cb": cb, "ck": ck,
    }
    nc = _bacc.Bacc("TRN2", target_bir_lowering=False, num_devices=1)
    args = [nc.dram_tensor(f"{k}_dram", a.shape, _mybir.dt.from_np(a.dtype), kind="ExternalInput").ap()
            for k, a in arrays.items()]
    out = nc.dram_tensor("out_dram", (N, D), _mybir.dt.float32, kind="ExternalOutput").ap()
    build_kernel(nc, *args, out)
    r = _run(nc, [{f"{k}_dram": a for k, a in arrays.items()}], core_ids=[0])
    return r.results[0]["out_dram"].reshape(B, L1, D)
```
